# Optimizing a Trainium2 kernel written in Bass

```python
import numpy as np
import jax
import jax.numpy as jnp

def _softmax(x, axis=-1):
    return jax.nn.softmax(x, axis=axis)

def _gelu(x):
    return jax.nn.gelu(x, approximate=True)

def _silu(x):
    return jax.nn.silu(x)

def _sigmoid(x):
    return jax.nn.sigmoid(x)

def _layernorm(x, axis=-1, eps=1e-05):
    m = jnp.mean(x, axis=axis, keepdims=True)
    v = jnp.var(x, axis=axis, keepdims=True)
    return (x - m) / jnp.sqrt(v + eps)

def _scatter_add(tgt, idx, src, axis=0):
    return tgt.at[idx].add(src)

def _segment_sum(src, seg, n):
    return jax.ops.segment_sum(src, seg, n)
kernel_name = 'mk_adj_resnorm_d2_adj_r2_b9aadf'

def setup_inputs(seed: int=0):
    np.random.seed(seed)
    _w = jnp.asarray

    def _rec_inputs():
        import jax
        import jax.numpy as jnp
        _gk = jax.random.key(seed)
        x = 7.22e-05 + 1 * jax.random.normal(jax.random.fold_in(_gk, 1), (16, 512, 256), jnp.float32)
        _a = jax.random.bernoulli(jax.random.fold_in(_gk, 2), 0.00390625, (16, 512, 512))
        _a = jnp.logical_or(_a, jnp.swapaxes(_a, -1, -2))
        _a = jnp.logical_or(_a, jnp.eye(512, dtype=bool))
        _af = _a.astype(jnp.float32)
        _af = _af * jax.random.uniform(jax.random.fold_in(_gk, 3), (16, 512, 512), jnp.float32, 0.05, 1)
        adj = _af
        return (x, adj)
    x, adj = _rec_inputs()

    def _L0_gnn_setup():
        import jax, jax.numpy as jnp
        import numpy as np
        key = jax.random.key(seed)
        k1, k2, k3 = jax.random.split(key, 3)
        B, N, F, D = (8, 1024, 256, 256)
        x = jax.random.normal(k1, (B, N, F), dtype=jnp.float32)
        a = jax.random.uniform(k2, (B, N, N), dtype=jnp.float32)
        kernel = jax.random.normal(k3, (F, D), dtype=jnp.float32) * (1.0 / np.sqrt(F))
        return {'x': x, 'a': a, 'kernel': kernel}
    _L0_gnn_all = _L0_gnn_setup()
    _L0_gnn_in = {k: v for k, v in _L0_gnn_all.items() if k in ('kernel',)}
    del _L0_gnn_all

    def _L1_gnn_setup():
        import jax, jax.numpy as jnp
        import numpy as np
        B, N, D = (8, 1024, 256)
        key = jax.random.key(seed)
        ks = jax.random.split(key, 8)
        scale = 0.5 / np.sqrt(D)
        x = jax.random.normal(ks[0], (B, N, D), dtype=jnp.float32)
        adj = jax.random.uniform(ks[1], (B, N, N), dtype=jnp.float32)
        Wq_w = jax.random.normal(ks[2], (D, D), dtype=jnp.float32) * scale
        Wk_w = jax.random.normal(ks[3], (D, D), dtype=jnp.float32) * scale
        Wv_w = jax.random.normal(ks[4], (D, D), dtype=jnp.float32) * scale
        Wq_b = jnp.zeros((D,), dtype=jnp.float32)
        Wk_b = jnp.zeros((D,), dtype=jnp.float32)
        Wv_b = jnp.zeros((D,), dtype=jnp.float32)
        return {'x': x, 'adj': adj, 'Wq_w': Wq_w, 'Wq_b': Wq_b, 'Wk_w': Wk_w, 'Wk_b': Wk_b, 'Wv_w': Wv_w, 'Wv_b': Wv_b}
    _L1_gnn_all = _L1_gnn_setup()
    _L1_gnn_in = {k: v for k, v in _L1_gnn_all.items() if k in ('Wq_w', 'Wq_b', 'Wk_w', 'Wk_b', 'Wv_w', 'Wv_b')}
    del _L1_gnn_all
    return {'x': x, 'adj': adj, 'L0_gnn_kernel': _L0_gnn_in['kernel'], 'L1_gnn_Wq_w': _L1_gnn_in['Wq_w'], 'L1_gnn_Wq_b': _L1_gnn_in['Wq_b'], 'L1_gnn_Wk_w': _L1_gnn_in['Wk_w'], 'L1_gnn_Wk_b': _L1_gnn_in['Wk_b'], 'L1_gnn_Wv_w': _L1_gnn_in['Wv_w'], 'L1_gnn_Wv_b': _L1_gnn_in['Wv_b']}

def reference(x, adj, L0_gnn_kernel, L1_gnn_Wq_w, L1_gnn_Wq_b, L1_gnn_Wk_w, L1_gnn_Wk_b, L1_gnn_Wv_w, L1_gnn_Wv_b):
    import jax
    import jax.numpy as jnp

    def _L0_gnn_ref(x, a, kernel):
        import jax, jax.numpy as jnp
        import numpy as np
        t = jnp.einsum('bnm,bmf->bnf', a, x)
        out = jnp.einsum('bnf,fd->bnd', t, kernel)
        out = jax.nn.relu(out)
        mask = (jnp.sum((x != 0).astype(jnp.float32), axis=-1, keepdims=True) > 0).astype(jnp.float32)
        return out * mask

    def _L1_gnn_ref(x, adj, Wq_w, Wq_b, Wk_w, Wk_b, Wv_w, Wv_b):
        import jax, jax.numpy as jnp
        import numpy as np
        B, N, D = (8, 1024, 256)
        query = jnp.einsum('bnd,od->bno', x, Wq_w) + Wq_b
        keyt = jnp.einsum('bnd,od->bno', x, Wk_w) + Wk_b
        value = jnp.einsum('bnd,od->bno', x, Wv_w) + Wv_b
        weight = jnp.einsum('bqd,bkd->bqk', query, keyt)
        weight = adj * jnp.exp(weight)
        weight = weight / jnp.sum(weight, axis=2, keepdims=True)
        return jnp.einsum('bqk,bkd->bqd', weight, value)
    x = _layernorm(x + _L0_gnn_ref(x, adj, L0_gnn_kernel), axis=-1)
    x = _layernorm(x + _L1_gnn_ref(x, adj, L1_gnn_Wq_w, L1_gnn_Wq_b, L1_gnn_Wk_w, L1_gnn_Wk_b, L1_gnn_Wv_w, L1_gnn_Wv_b), axis=-1)
    return x

_drawn_inputs = setup_inputs


def setup_inputs(seed=0):
    import zlib

    import numpy as np

    out = dict(_drawn_inputs(seed))
    spreads = {'L1_gnn_Wq_b': (0.0, 0.1), 'L1_gnn_Wk_b': (0.0, 0.1), 'L1_gnn_Wv_b': (0.0, 0.1)}
    factors = {}
    for name, (base, spread) in spreads.items():
        noise = np.random.default_rng([zlib.crc32(name.encode()), seed]).standard_normal(out[name].shape)
        drawn = base * np.exp(spread * noise) if base else spread * noise
        out[name] = jnp.asarray(drawn.astype(out[name].dtype))
    for name, factor in factors.items():
        out[name] = (out[name] * factor).astype(out[name].dtype)
    return out
```

```python
import concourse.bass as bass
from concourse import mybir
from contextlib import ExitStack

P = 128
GRAPHS = 16
NODES = 512
FEATURES = 256
BLOCKS = NODES // P
CHUNKS = FEATURES // P
HALF = NODES // 2
VCOLS = FEATURES + 2
BANK = 512
EPS = 1e-5


def build(nc, x, adj_t, w0, wq, wk, wv_t, bq_rep, bq_col, bk_col, bv_rep, identity, out):
    f32, f32r = mybir.dt.float32, mybir.dt.float32r
    ALU, ACT, AX = mybir.AluOpType, mybir.ActivationFunctionType, mybir.AxisListType

    with ExitStack() as ctx:
        def sbuf(name, shape, dtype=f32):
            return ctx.enter_context(nc.sbuf_tensor(name, shape, dtype))

        def sem(name):
            return ctx.enter_context(nc.semaphore(name))

        adj = sbuf("adj", [P, 2, BLOCKS, NODES])
        xin = sbuf("xin", [P, 2, BLOCKS, FEATURES])
        adj_h = sbuf("adj_h", [P, BLOCKS, NODES], f32r)
        adj_l = sbuf("adj_l", [P, BLOCKS, NODES], f32r)
        x_h = sbuf("x_h", [P, BLOCKS, FEATURES], f32r)
        x_l = sbuf("x_l", [P, BLOCKS, FEATURES], f32r)
        t_h = sbuf("t_h", [P, 2, CHUNKS, HALF], f32r)
        t_l = sbuf("t_l", [P, 2, CHUNKS, HALF], f32r)
        r = sbuf("r", [P, BLOCKS, FEATURES])
        x1 = sbuf("x1", [P, BLOCKS, FEATURES])
        x1b = sbuf("x1b", [P, BLOCKS, FEATURES])
        x1t_h = sbuf("x1t_h", [P, CHUNKS, NODES], f32r)
        x1t_l = sbuf("x1t_l", [P, CHUNKS, NODES], f32r)
        y_h = sbuf("y_h", [P, CHUNKS, NODES], f32r)
        y_l = sbuf("y_l", [P, CHUNKS, NODES], f32r)
        v_h = sbuf("v_h", [P, BLOCKS, VCOLS], f32r)
        v_l = sbuf("v_l", [P, BLOCKS, VCOLS], f32r)
        c_key = sbuf("c_key", [P, BLOCKS])
        expo = sbuf("expo", [P, BLOCKS, NODES])
        wgt = sbuf("wgt", [P, BLOCKS, NODES])
        wgt_h = sbuf("wgt_h", [P, BLOCKS, NODES], f32r)
        wgt_l = sbuf("wgt_l", [P, BLOCKS, NODES], f32r)
        u = sbuf("u", [P, BLOCKS, FEATURES])
        yout = sbuf("yout", [P, 2, BLOCKS, FEATURES])
        xmax = sbuf("xmax", [P, BLOCKS])
        mask = sbuf("mask", [P, BLOCKS])
        neg_half = sbuf("neg_half", [P, BLOCKS])
        stats1 = sbuf("stats1", [P, BLOCKS, 6])
        mv1 = sbuf("mv1", [P, BLOCKS, 2])
        var1 = sbuf("var1", [P, BLOCKS])
        rstd1 = sbuf("rstd1", [P, BLOCKS])
        mrstd1 = sbuf("mrstd1", [P, BLOCKS])
        rsum = sbuf("rsum", [P, BLOCKS])
        stats2 = sbuf("stats2", [P, BLOCKS, 6])
        mv2 = sbuf("mv2", [P, BLOCKS, 2])
        var2 = sbuf("var2", [P, BLOCKS])
        rstd2 = sbuf("rstd2", [P, BLOCKS])
        shift2 = sbuf("shift2", [P, BLOCKS])
        ident = sbuf("ident", [P, P])
        w0_f = sbuf("w0_f", [P, CHUNKS, FEATURES])
        w0_h = sbuf("w0_h", [P, CHUNKS, FEATURES], f32r)
        w0_l = sbuf("w0_l", [P, CHUNKS, FEATURES], f32r)
        wq_f = sbuf("wq_f", [P, CHUNKS, FEATURES])
        wk_f = sbuf("wk_f", [P, CHUNKS, FEATURES])
        wv_f = sbuf("wv_f", [P, CHUNKS, VCOLS])
        wv_h = sbuf("wv_h", [P, CHUNKS, VCOLS], f32r)
        wv_l = sbuf("wv_l", [P, CHUNKS, VCOLS], f32r)
        wqk_h = sbuf("wqk_h", [P, CHUNKS, FEATURES], f32r)
        wqk_l = sbuf("wqk_l", [P, CHUNKS, FEATURES], f32r)
        bqr = sbuf("bqr", [P, CHUNKS, P])
        bqc = sbuf("bqc", [P, CHUNKS])
        bkc = sbuf("bkc", [P, CHUNKS])
        bv = sbuf("bv", [P, FEATURES])
        y_bias = sbuf("y_bias", [P, CHUNKS])
        bqbk = sbuf("bqbk", [P, 1])

        psum = ctx.enter_context(nc.psum_tensor("psum", [P, 8, BANK], f32))
        Y_BANK = [0, 1]
        V_BANK = 2
        S_BANK = [6, 7, 0, 1]
        T_BANK = [2, 3]
        O_BANK = [4, 5]
        X1T_BANK = [4, 5]
        Q_BANK = [6, 7, 3, 2]

        x_in = [sem("x_in0"), sem("x_in1")]
        adj_in = [sem("adj_in0"), sem("adj_in1")]
        adj0_in = [sem(f"adj0_in{k}") for k in range(BLOCKS)]
        stored = [sem("stored0"), sem("stored1")]
        w0_in, wqk_in, wv_in, bv_in, id_in = (sem(n) for n in ("w0_in", "wqk_in", "wv_in", "bv_in", "id_in"))
        const_set, w0_split = sem("const_set"), sem("w0_split")
        fold_mm, fold_out, fold_split = sem("fold_mm"), sem("fold_out"), sem("fold_split")
        xh_out, xl_out = sem("xh_out"), sem("xl_out")
        adjh_out, adjl_out = sem("adjh_out"), sem("adjl_out")
        t_mm, th_out, tl_out = sem("t_mm"), sem("th_out"), sem("tl_out")
        o_mm, r_out = sem("o_mm"), sem("r_out")
        mask_max, mask_out = sem("mask_max"), sem("mask_out")
        mv1_out, var1_out = sem("mv1_out"), sem("var1_out")
        rstd1_out, mrstd1_out = sem("rstd1_out"), sem("mrstd1_out")
        x1_out, x1b_out = sem("x1_out"), sem("x1b_out")
        x1t_mm, x1th_out, x1tl_out = sem("x1t_mm"), sem("x1th_out"), sem("x1tl_out")
        y_mm, yh_out, yl_out = sem("y_mm"), sem("yh_out"), sem("yl_out")
        v_mm, vh_out, vl_out = sem("v_mm"), sem("vh_out"), sem("vl_out")
        c_out = sem("c_out")
        s_mm, exp_out = sem("s_mm"), sem("exp_out")
        wgt_out, wgth_out, wgtl_out = sem("wgt_out"), sem("wgth_out"), sem("wgtl_out")
        q_mm, rsum_out, u_out = sem("q_mm"), sem("rsum_out"), sem("u_out")
        mv2_out, var2_out, rstd2_out, shift2_out = sem("mv2_out"), sem("var2_out"), sem("rstd2_out"), sem("shift2_out")
        norm_out = sem("norm_out")

        def reach(engine, semaphore, i, m, each, nth):
            value = m * each + nth
            if isinstance(i, int):
                if i * each + value > 0:
                    engine.wait_ge(semaphore, i * each + value)
            else:
                engine.wait_ge(semaphore, i * each + value)

        def reach_dma(engine, by_parity, i, m, earlier=0):
            value = 16 * (m // 2 + 1 - earlier)
            if isinstance(i, int):
                if 8 * i + value > 0:
                    engine.wait_ge(by_parity[m % 2], 8 * i + value)
            else:
                engine.wait_ge(by_parity[m % 2], i * 8 + value)

        def exists(i, m):
            return not isinstance(i, int) or 0 <= i + m < GRAPHS

        def each_turn(engine, turn):
            for b in range(-1, 2):
                turn(0, b)
            with engine.Fori(1, GRAPHS // 2 - 1) as pair:
                for m in range(2):
                    turn(pair * 2, m)
            for b in range(GRAPHS - 2, GRAPHS + 1):
                turn(0, b)

        def graph(dram, i, m):
            return dram[bass.ds(i + m, 1), :, :].rearrange("g p n -> (g p) n")

        def passes(high, low, moving_high, moving_low):
            return ((high, moving_high), (high, moving_low), (low, moving_high))

        block = ctx.enter_context(nc.Block())

        @block.sync
        def _(sp):
            def load_x(i, m):
                sp.dma_start(xin[:, m % 2].rearrange("p k f -> p (k f)"), graph(x, i, m)).then_inc(x_in[m % 2], 16)

            def load_adj(i, m):
                sp.dma_start(adj[:, m % 2].rearrange("p k n -> p (k n)"), graph(adj_t, i, m)).then_inc(adj_in[m % 2], 16)

            load_x(0, 0)
            for k in range(BLOCKS):
                sp.dma_start(adj[:, 0, k, :], adj_t[0, :, k * NODES:(k + 1) * NODES]).then_inc(adj0_in[k], 16)
            sp.dma_start(w0_f[:, :, :].rearrange("p k f -> p (k f)"), w0).then_inc(w0_in, 16)
            load_x(0, 1)
            load_adj(0, 1)

            def turn(i, m):
                if exists(i, m) and exists(i, m + 2):
                    reach(sp, r_out, i, m, 2, 2)
                    load_x(i, m + 2)
                if exists(i, m - 1):
                    reach(sp, norm_out, i, m - 1, 1, 1)
                    sp.dma_start(graph(out, i, m - 1), yout[:, (m - 1) % 2].rearrange("p k f -> p (k f)")
                                 ).then_inc(stored[(m - 1) % 2], 16)
                if exists(i, m) and exists(i, m + 2):
                    reach(sp, wgt_out, i, m, 4, 4)
                    load_adj(i, m + 2)

            each_turn(sp, turn)
            for parity in range(2):
                sp.wait_ge(stored[parity], 16 * GRAPHS // 2)

        @block.tensor
        def _(pe):
            pe.wait_ge(wqk_in, 16 * 5)
            for c in range(CHUNKS):
                rows = slice(c * P, (c + 1) * P)
                for o in range(CHUNKS):
                    nc.tensor.matmul(psum[:, 0, c * FEATURES:(c + 1) * FEATURES], wk_f[:, o, rows], wq_f[:, o, :],
                                     start=(o == 0), stop=(o == CHUNKS - 1))
            for c in range(CHUNKS):
                rows = slice(c * P, (c + 1) * P)
                for o in range(CHUNKS):
                    nc.tensor.matmul(psum[:, 1, c:c + 1], wq_f[:, o, rows], bkc[:, o:o + 1],
                                     start=(o == 0), stop=(o == CHUNKS - 1))
                for o in range(CHUNKS):
                    nc.tensor.matmul(psum[:, 1, 2 + c:3 + c], wk_f[:, o, rows], bqc[:, o:o + 1],
                                     start=(o == 0), stop=(o == CHUNKS - 1))
            for o in range(CHUNKS):
                last = nc.tensor.matmul(psum[:, 1, 4:5], bqr[:, o, :], bkc[:, o:o + 1],
                                        start=(o == 0), stop=(o == CHUNKS - 1))
            last.then_inc(fold_mm, 1)

            def make_y(i, m):
                reach(pe, x1th_out, i, m, 2, 2)
                for fo in range(CHUNKS):
                    bank = psum[:, Y_BANK[fo], :]
                    cols = slice(fo * P, (fo + 1) * P)
                    for n, (w, mv) in enumerate(((wqk_h, x1t_h), (wqk_l, x1t_h), (wqk_h, x1t_l))):
                        if fo == 0 and n == 2:
                            reach(pe, x1tl_out, i, m, 2, 2)
                        for c in range(CHUNKS):
                            last = nc.tensor.matmul(bank, w[:, c, cols], mv[:, c, :], start=(n == 0 and c == 0),
                                                    stop=(n == 2 and c == CHUNKS - 1))
                    last.then_inc(y_mm, 1)

            def make_v(i, m):
                reach(pe, u_out, i, m - 1, 4, 4)
                for k in range(BLOCKS):
                    rows = slice(k * P, (k + 1) * P)
                    for n, (st, mv) in enumerate(passes(x1t_h, x1t_l, wv_h, wv_l)):
                        for c in range(CHUNKS):
                            last = nc.tensor.matmul(psum[:, V_BANK + k, 0:VCOLS], st[:, c, rows], mv[:, c, :],
                                                    start=(n == 0 and c == 0), stop=(n == 2 and c == CHUNKS - 1))
                    if k % 2:
                        last.then_inc(v_mm, 1)

            def make_scores(i, m):
                reach(pe, yh_out, i, m, 2, 2)
                reach(pe, yl_out, i, m, 2, 2)
                for k in range(BLOCKS):
                    rows = slice(k * P, (k + 1) * P)
                    for n, (st, mv) in enumerate(passes(y_h, y_l, x1t_h, x1t_l)):
                        for c in range(CHUNKS):
                            last = nc.tensor.matmul(psum[:, S_BANK[k], :], st[:, c, rows], mv[:, c, :],
                                                    start=(n == 0 and c == 0), stop=(n == 2 and c == CHUNKS - 1))
                    last.then_inc(s_mm, 1)

            def make_t(i, m):
                reach(pe, xh_out, i, m, 1, 1)
                reach(pe, xl_out, i, m, 1, 1)
                reach(pe, vl_out, i, m - 1, 2, 2)
                for half in range(2):
                    nodes = slice(half * HALF, (half + 1) * HALF)
                    for f in range(CHUNKS):
                        cols = slice(f * P, (f + 1) * P)
                        for k in range(BLOCKS):
                            if half == 0 and f == 0:
                                reach(pe, adjh_out, i, m, 4, k + 1)
                                reach(pe, adjl_out, i, m, 4, k + 1)
                            for n, (st, mv) in enumerate(passes(x_h, x_l, adj_h, adj_l)):
                                last = nc.tensor.matmul(psum[:, T_BANK[half], f * HALF:(f + 1) * HALF],
                                                        st[:, k, cols], mv[:, k, nodes],
                                                        start=(k == 0 and n == 0), stop=(k == BLOCKS - 1 and n == 2))
                    last.then_inc(t_mm, 1)

            def make_o(i, m):
                for half in range(2):
                    reach(pe, th_out, i, m, 2, half + 1)
                    reach(pe, tl_out, i, m, 2, half + 1)
                    for k in range(2):
                        rows = slice(k * P, (k + 1) * P)
                        for n, (st, mv) in enumerate(passes(t_h, t_l, w0_h, w0_l)):
                            for c in range(CHUNKS):
                                last = nc.tensor.matmul(psum[:, O_BANK[half], k * FEATURES:(k + 1) * FEATURES],
                                                        st[:, half, c, rows], mv[:, c, :],
                                                        start=(n == 0 and c == 0), stop=(n == 2 and c == CHUNKS - 1))
                    last.then_inc(o_mm, 1)

            def make_attention(i, m, q):
                if q == 0:
                    reach(pe, vh_out, i, m, 2, 2)
                    reach(pe, vl_out, i, m, 2, 2)
                rows = slice(q * P, (q + 1) * P)
                for k in range(BLOCKS):
                    if q == 0:
                        reach(pe, wgth_out, i, m, 4, k + 1)
                        reach(pe, wgtl_out, i, m, 4, k + 1)
                    for n, (st, mv) in enumerate(passes(wgt_h, wgt_l, v_h, v_l)):
                        last = nc.tensor.matmul(psum[:, Q_BANK[q], 0:VCOLS], st[:, k, rows], mv[:, k, :],
                                                start=(k == 0 and n == 0), stop=(k == BLOCKS - 1 and n == 2))
                last.then_inc(q_mm, 1)

            def make_x1t(i, m):
                for k in range(BLOCKS):
                    if k % 2 == 0:
                        reach(pe, x1_out, i, m, 2, k // 2 + 1)
                    for c in range(CHUNKS):
                        last = nc.tensor.transpose(psum[:, X1T_BANK[c], k * P:(k + 1) * P],
                                                   x1[:, k, c * P:(c + 1) * P], ident[:, :])
                last.then_inc(x1t_mm, 1)

            def turn(i, m):
                if exists(i, m):
                    if isinstance(i, int) and i + m == 0:
                        pe.wait_ge(fold_split, 4)
                    make_y(i, m)
                    make_v(i, m)
                    make_scores(i, m)
                if exists(i, m + 1):
                    make_t(i, m + 1)
                    if isinstance(i, int) and i + m == -1:
                        pe.wait_ge(w0_split, 2)
                    make_o(i, m + 1)
                if exists(i, m):
                    for q in range(3):
                        make_attention(i, m, q)
                if exists(i, m + 1):
                    if isinstance(i, int) and i + m == -1:
                        pe.wait_ge(id_in, 16)
                    make_x1t(i, m + 1)
                if exists(i, m):
                    make_attention(i, m, 3)

            each_turn(pe, turn)

        @block.scalar
        def _(act):
            flat = lambda t: t[:, :, :].rearrange("p a b -> p (a b)")
            act.dma_start(flat(wk_f), wk).then_inc(wqk_in, 16)
            act.dma_start(flat(wq_f), wq).then_inc(wqk_in, 16)
            act.dma_start(bkc[:, :], bk_col).then_inc(wqk_in, 16)
            act.dma_start(bqc[:, :], bq_col).then_inc(wqk_in, 16)
            act.dma_start(flat(bqr), bq_rep).then_inc(wqk_in, 16)
            act.dma_start(flat(wv_f), wv_t).then_inc(wv_in, 16)
            act.dma_start(ident[:, :], identity).then_inc(id_in, 16)
            act.dma_start(bv[:, :], bv_rep).then_inc(bv_in, 16)

            def split_x(i, m):
                reach_dma(act, x_in, i, m)
                nc.scalar.activation(flat(x_h), xin[:, m % 2].rearrange("p k f -> p (k f)"), ACT.Copy).then_inc(xh_out, 1)

            def split_adj(i, m, k):
                if isinstance(i, int) and i + m == 0:
                    act.wait_ge(adj0_in[k], 16)
                elif k == 0:
                    reach_dma(act, adj_in, i, m, earlier=(m + 1) % 2)
                nc.scalar.activation(adj_h[:, k, :], adj[:, m % 2, k, :], ACT.Copy).then_inc(adjh_out, 1)

            split_x(0, 0)

            def turn(i, m):
                now, after = exists(i, m), exists(i, m + 1)
                if after:
                    split_adj(i, m + 1, 0)
                    split_adj(i, m + 1, 1)
                if isinstance(i, int) and i + m == -1:
                    act.wait_ge(w0_in, 16)
                    nc.scalar.activation(flat(w0_h), flat(w0_f), ACT.Copy).then_inc(w0_split, 1)
                    act.wait_ge(fold_mm, 1)
                    nc.scalar.activation(flat(wqk_h), psum[:, 0, :], ACT.Copy).then_inc(fold_split, 1)
                    act.wait_ge(fold_out, 3)
                    nc.scalar.activation(flat(wv_h), flat(wv_f), ACT.Copy).then_inc(fold_split, 1)
                for fo in range(CHUNKS):
                    if now:
                        if isinstance(i, int) and i + m == 0 and fo == 0:
                            act.wait_ge(fold_out, 3)
                        reach(act, y_mm, i, m, 2, fo + 1)
                        nc.scalar.activation(y_h[:, fo, :], psum[:, Y_BANK[fo], :], ACT.Identity,
                                             bias=y_bias[:, fo:fo + 1]).then_inc(yh_out, 1)
                    if after:
                        split_adj(i, m + 1, 2 + fo)
                if now:
                    for pair in range(2):
                        reach(act, v_mm, i, m, 2, pair + 1)
                        nc.scalar.activation(v_h[:, 2 * pair:2 * pair + 2, 0:FEATURES],
                                             psum[:, V_BANK + 2 * pair:V_BANK + 2 * pair + 2, 0:FEATURES],
                                             ACT.Copy).then_inc(vh_out, 1)
                if exists(i, m - 1):
                    reach(act, shift2_out, i, m - 1, 1, 1)
                    reach_dma(act, stored, i, m - 3)
                    for k in range(BLOCKS):
                        last = nc.scalar.activation(yout[:, (m - 1) % 2, k, :], u[:, k, :], ACT.Identity,
                                                    bias=shift2[:, k:k + 1], scale=rstd2[:, k:k + 1])
                    last.then_inc(norm_out, 1)

                def split_weights(k):
                    reach(act, wgt_out, i, m, 4, k + 1)
                    nc.scalar.activation(wgt_h[:, k, :], wgt[:, k, :], ACT.Copy).then_inc(wgth_out, 1)

                if now:
                    reach(act, c_out, i, m, 1, 1)
                    for k in range(BLOCKS):
                        reach(act, s_mm, i, m, 4, k + 1)
                        nc.scalar.activation(expo[:, k, :], psum[:, S_BANK[k], :], ACT.Exp,
                                             bias=c_key[:, k:k + 1]).then_inc(exp_out, 1)
                        if k:
                            split_weights(k - 1)
                    split_weights(BLOCKS - 1)
                if after:
                    for half in range(2):
                        reach(act, t_mm, i, m + 1, 2, half + 1)
                        nc.scalar.activation(t_h[:, half].rearrange("p c n -> p (c n)"), psum[:, T_BANK[half], :],
                                             ACT.Copy).then_inc(th_out, 1)
                if exists(i, m + 2) and exists(i, m + 1):
                    split_x(i, m + 2)
                if after:
                    reach(act, x1t_mm, i, m + 1, 1, 1)
                    for c in range(CHUNKS):
                        nc.scalar.activation(x1t_h[:, c, :], psum[:, X1T_BANK[c], :], ACT.Copy).then_inc(x1th_out, 1)

            each_turn(act, turn)

        @block.vector
        def _(dve):
            flat = lambda t: t[:, :, :].rearrange("p a b -> p (a b)")
            as32 = lambda ap: ap.bitcast(f32)

            nc.vector.memset(neg_half[:, :], -0.5).then_inc(const_set, 1)
            nc.vector.memset(as32(v_h[:, :, FEATURES:FEATURES + 1]), 1.0)
            nc.vector.memset(as32(v_h[:, :, FEATURES + 1:VCOLS]), 0.0)
            nc.vector.memset(as32(v_l[:, :, FEATURES:VCOLS]), 0.0)

            def find_mask(i, m):
                reach_dma(dve, x_in, i, m)
                nc.vector.tensor_reduce(xmax[:, :], xin[:, m % 2], AX.X, ALU.max,
                                        apply_absolute_value=True).then_inc(mask_max, 1)
                reach(dve, mask_max, i, m, 1, 1)
                nc.vector.tensor_scalar(mask[:, :], xmax[:, :], 0.0, None, ALU.is_gt).then_inc(mask_out, 1)

            def add_attention(i, m, q):
                reach(dve, q_mm, i, m, 4, q + 1)
                nc.vector.reciprocal(rsum[:, q:q + 1], psum[:, Q_BANK[q], FEATURES:FEATURES + 1]).then_inc(rsum_out, 1)
                if q == 0:
                    reach(dve, x1b_out, i, m, 1, 1)
                reach(dve, rsum_out, i, m, 4, q + 1)
                nc.vector.scalar_tensor_tensor(u[:, q, :], psum[:, Q_BANK[q], 0:FEATURES], rsum[:, q:q + 1],
                                               x1b[:, q, :], ALU.mult, ALU.add).then_inc(u_out, 1)
                reach(dve, u_out, i, m, 4, q + 1)
                nc.vector.bn_stats(stats2[:, q, :], u[:, q, :])

            def turn(i, m):
                now, after = exists(i, m), exists(i, m + 1)
                if exists(i, m - 1):
                    add_attention(i, m - 1, 3)
                    dve.drain()
                    for k in range(BLOCKS):
                        last = nc.vector.bn_aggr(mv2[:, k, :], stats2[:, k, :])
                    last.then_inc(mv2_out, 1)
                    reach(dve, mv2_out, i, m - 1, 1, 1)
                    nc.vector.tensor_scalar(var2[:, :], mv2[:, :, 1], EPS, None, ALU.add).then_inc(var2_out, 1)
                if isinstance(i, int) and i + m == -1:
                    dve.wait_ge(w0_split, 1)
                    nc.vector.tensor_tensor(flat(w0_l), flat(w0_f), as32(flat(w0_h)), ALU.subtract).then_inc(w0_split, 1)
                    dve.wait_ge(fold_mm, 1)
                    nc.vector.tensor_copy(y_bias[:, :], psum[:, 1, 0:2]).then_inc(fold_out, 1)
                    nc.vector.tensor_copy(bqbk[:, :], psum[:, 1, 4:5]).then_inc(fold_out, 1)
                    dve.wait_ge(wv_in, 16)
                    nc.vector.tensor_copy(wv_f[:, :, FEATURES], psum[:, 1, 2:4]).then_inc(fold_out, 1)
                    dve.wait_ge(fold_split, 2)
                    nc.vector.tensor_tensor(flat(wqk_l), psum[:, 0, :], as32(flat(wqk_h)), ALU.subtract).then_inc(fold_split, 1)
                    nc.vector.tensor_tensor(flat(wv_l), flat(wv_f), as32(flat(wv_h)), ALU.subtract).then_inc(fold_split, 1)
                for fo in range(CHUNKS):
                    if now:
                        reach(dve, yh_out, i, m, 2, fo + 1)
                        nc.vector.scalar_tensor_tensor(y_l[:, fo, :], psum[:, Y_BANK[fo], :], y_bias[:, fo:fo + 1],
                                                       as32(y_h[:, fo, :]), ALU.add, ALU.subtract).then_inc(yl_out, 1)
                    if fo == 0 and exists(i, m - 1):
                        reach(dve, rstd2_out, i, m - 1, 1, 1)
                        nc.vector.scalar_tensor_tensor(shift2[:, :], mv2[:, :, 0], -1.0, rstd2[:, :],
                                                       ALU.mult, ALU.mult).then_inc(shift2_out, 1)
                if now:
                    for pair in range(2):
                        reach(dve, vh_out, i, m, 2, pair + 1)
                        if pair == 1:
                            nc.vector.tensor_scalar(c_key[:, :], psum[:, V_BANK:V_BANK + BLOCKS, FEATURES],
                                                    bqbk[:, 0:1], None, ALU.add).then_inc(c_out, 1)
                        nc.vector.tensor_tensor(v_l[:, 2 * pair:2 * pair + 2, 0:FEATURES],
                                                psum[:, V_BANK + 2 * pair:V_BANK + 2 * pair + 2, 0:FEATURES],
                                                as32(v_h[:, 2 * pair:2 * pair + 2, 0:FEATURES]),
                                                ALU.subtract).then_inc(vl_out, 1)
                if after:
                    find_mask(i, m + 1)

                def split_weights(k):
                    reach(dve, wgth_out, i, m, 4, k + 1)
                    nc.vector.tensor_tensor(wgt_l[:, k, :], wgt[:, k, :], as32(wgt_h[:, k, :]),
                                            ALU.subtract).then_inc(wgtl_out, 1)

                if now:
                    for k in range(BLOCKS):
                        reach(dve, exp_out, i, m, 4, k + 1)
                        nc.vector.tensor_tensor(wgt[:, k, :], expo[:, k, :], adj[:, m % 2, k, :],
                                                ALU.mult).then_inc(wgt_out, 1)
                        if k:
                            split_weights(k - 1)
                    split_weights(BLOCKS - 1)
                if after:
                    for half in range(2):
                        reach(dve, th_out, i, m + 1, 2, half + 1)
                        nc.vector.tensor_tensor(t_l[:, half].rearrange("p c n -> p (c n)"), psum[:, T_BANK[half], :],
                                                as32(t_h[:, half].rearrange("p c n -> p (c n)")),
                                                ALU.subtract).then_inc(tl_out, 1)
                    for half in range(2):
                        blocks = slice(2 * half, 2 * half + 2)
                        reach(dve, o_mm, i, m + 1, 2, half + 1)
                        nc.vector.scalar_tensor_tensor(r[:, blocks, :].rearrange("p k f -> p (k f)"),
                                                       psum[:, O_BANK[half], :], 0.0,
                                                       xin[:, (m + 1) % 2, blocks, :].rearrange("p k f -> p (k f)"),
                                                       ALU.max, ALU.add).then_inc(r_out, 1)
                        reach(dve, r_out, i, m + 1, 2, half + 1)
                        for k in (2 * half, 2 * half + 1):
                            nc.vector.bn_stats(stats1[:, k, :], r[:, k, :])
                        dve.drain()
                        for k in (2 * half, 2 * half + 1):
                            last = nc.vector.bn_aggr(mv1[:, k, :], stats1[:, k, :])
                        last.then_inc(mv1_out, 1)
                        reach(dve, mv1_out, i, m + 1, 2, half + 1)
                        nc.vector.tensor_scalar(var1[:, blocks], mv1[:, blocks, 1], EPS, None, ALU.add).then_inc(var1_out, 1)
                    reach(dve, mask_out, i, m + 1, 1, 1)
                    reach(dve, x1b_out, i, m, 1, 1)
                    for half in range(2):
                        blocks = slice(2 * half, 2 * half + 2)
                        reach(dve, rstd1_out, i, m + 1, 2, half + 1)
                        nc.vector.tensor_tensor(mrstd1[:, blocks], rstd1[:, blocks], mask[:, blocks],
                                                ALU.mult).then_inc(mrstd1_out, 1)
                        reach(dve, mrstd1_out, i, m + 1, 2, half + 1)
                        for k in (2 * half, 2 * half + 1):
                            last = nc.vector.tensor_scalar(x1[:, k, :], r[:, k, :], mv1[:, k, 0:1],
                                                           mrstd1[:, k:k + 1], ALU.subtract, ALU.mult)
                        last.then_inc(x1_out, 1)
                        if now and half == 0:
                            add_attention(i, m, 0)
                if now and not after:
                    add_attention(i, m, 0)
                if now:
                    add_attention(i, m, 1)
                    add_attention(i, m, 2)
                if after:
                    for c in range(CHUNKS):
                        reach(dve, x1th_out, i, m + 1, 2, c + 1)
                        nc.vector.tensor_tensor(x1t_l[:, c, :], psum[:, X1T_BANK[c], :], as32(x1t_h[:, c, :]),
                                                ALU.subtract).then_inc(x1tl_out, 1)

            each_turn(dve, turn)

        @block.gpsimd
        def _(pool):
            flat = lambda t: t[:, :, :].rearrange("p a b -> p (a b)")
            as32 = lambda ap: ap.bitcast(f32)

            def split_x(i, m):
                reach(pool, xh_out, i, m, 1, 1)
                nc.gpsimd.tensor_tensor(flat(x_l), xin[:, m % 2].rearrange("p k f -> p (k f)"), as32(flat(x_h)),
                                        ALU.subtract).then_inc(xl_out, 1)

            pool.wait_ge(const_set, 1)
            split_x(0, 0)

            def turn(i, m):
                if exists(i, m - 1):
                    reach(pool, var2_out, i, m - 1, 1, 1)
                    nc.gpsimd.tensor_tensor(rstd2[:, :], var2[:, :], neg_half[:, :], ALU.pow).then_inc(rstd2_out, 1)
                if exists(i, m + 1):
                    for k in range(BLOCKS):
                        reach(pool, adjh_out, i, m + 1, 4, k + 1)
                        nc.gpsimd.tensor_tensor(adj_l[:, k, :], adj[:, (m + 1) % 2, k, :], as32(adj_h[:, k, :]),
                                                ALU.subtract).then_inc(adjl_out, 1)
                if exists(i, m):
                    if isinstance(i, int) and i + m == 0:
                        pool.wait_ge(bv_in, 16)
                    reach(pool, x1_out, i, m, 2, 2)
                    nc.gpsimd.tensor_tensor(x1b[:, :, :], x1[:, :, :],
                                            bv[:, :].unsqueeze(1).to_broadcast([P, BLOCKS, FEATURES]),
                                            ALU.add).then_inc(x1b_out, 1)
                if exists(i, m + 1):
                    for half in range(2):
                        blocks = slice(2 * half, 2 * half + 2)
                        reach(pool, var1_out, i, m + 1, 2, half + 1)
                        nc.gpsimd.tensor_tensor(rstd1[:, blocks], var1[:, blocks], neg_half[:, blocks],
                                                ALU.pow).then_inc(rstd1_out, 1)
                if exists(i, m + 2) and exists(i, m + 1):
                    split_x(i, m + 2)

            each_turn(pool, turn)


def kernel(x, adj, L0_gnn_kernel, L1_gnn_Wq_w, L1_gnn_Wq_b, L1_gnn_Wk_w, L1_gnn_Wk_b, L1_gnn_Wv_w, L1_gnn_Wv_b):
    import numpy as np
    import concourse.bacc as bacc
    from concourse import mybir as mb
    from concourse.bass_utils import run_bass_kernel_spmd

    def by_partition(a):
        a = np.asarray(a)
        *lead, rows, n = a.shape
        a = a.reshape(*lead, rows // P, P, n)
        return np.ascontiguousarray(np.moveaxis(a, -3, -2).reshape(*lead, P, rows // P * n))

    wv_t = np.asarray(L1_gnn_Wv_w).T
    wv_t = np.concatenate([wv_t, np.zeros((FEATURES, VCOLS - FEATURES), wv_t.dtype)], axis=1)
    bq = np.asarray(L1_gnn_Wq_b)[:, None]
    ins = {
        "x": by_partition(x),
        "adj_t": by_partition(np.swapaxes(np.asarray(adj), 1, 2)),
        "w0": by_partition(L0_gnn_kernel),
        "wq": by_partition(L1_gnn_Wq_w),
        "wk": by_partition(L1_gnn_Wk_w),
        "wv_t": by_partition(wv_t),
        "bq_rep": by_partition(np.repeat(bq, P, axis=1)),
        "bq_col": by_partition(bq),
        "bk_col": by_partition(np.asarray(L1_gnn_Wk_b)[:, None]),
        "bv_rep": np.ascontiguousarray(np.repeat(np.asarray(L1_gnn_Wv_b)[None, :], P, axis=0)),
        "identity": np.eye(P, dtype=np.float32),
    }
    nc = bacc.Bacc("TRN2", target_bir_lowering=False, num_devices=1)
    args = [nc.dram_tensor(f"in_{n}", a.shape, mb.dt.from_np(a.dtype), kind="ExternalInput").ap() for n, a in ins.items()]
    out = nc.dram_tensor("out", (GRAPHS, P, BLOCKS * FEATURES), mb.dt.float32, kind="ExternalOutput").ap()
    build(nc, *args, out)
    got = run_bass_kernel_spmd(nc, [{f"in_{n}": a for n, a in ins.items()}], core_ids=[0]).results[0]["out"]
    return np.ascontiguousarray(
        got.reshape(GRAPHS, P, BLOCKS, FEATURES).transpose(0, 2, 1, 3).reshape(GRAPHS, NODES, FEATURES))
```

```python
import concourse.bass as bass
from concourse import mybir
from contextlib import ExitStack

P = 128
GRAPHS = 16
NODES = 512
FEATURES = 256
BLOCKS = NODES // P
CHUNKS = FEATURES // P
HALF = NODES // 2
VCOLS = FEATURES + 2
BANK = 512
EPS = 1e-5


def build(nc, x, adj_t, w0, wq_bq, wk, wv_t, bq_rep, bk_col, bv_rep, identity, out):
    f32, f32r = mybir.dt.float32, mybir.dt.float32r
    ALU, ACT, AX = mybir.AluOpType, mybir.ActivationFunctionType, mybir.AxisListType

    with ExitStack() as ctx:
        def sbuf(name, shape, dtype=f32):
            return ctx.enter_context(nc.sbuf_tensor(name, shape, dtype))

        def sem(name):
            return ctx.enter_context(nc.semaphore(name))

        adj = sbuf("adj", [P, 2, BLOCKS, NODES])
        xin = sbuf("xin", [P, 2, BLOCKS, FEATURES])
        adj_h = sbuf("adj_h", [P, BLOCKS, NODES], f32r)
        adj_l = sbuf("adj_l", [P, BLOCKS, NODES], f32r)
        x_h = sbuf("x_h", [P, BLOCKS, FEATURES], f32r)
        x_l = sbuf("x_l", [P, BLOCKS, FEATURES], f32r)
        t_h = sbuf("t_h", [P, 2, CHUNKS, HALF], f32r)
        t_l = sbuf("t_l", [P, 2, CHUNKS, HALF], f32r)
        r = sbuf("r", [P, BLOCKS, FEATURES])
        x1 = sbuf("x1", [P, BLOCKS, FEATURES])
        x1b = sbuf("x1b", [P, BLOCKS, FEATURES])
        x1t_h = sbuf("x1t_h", [P, CHUNKS, NODES], f32r)
        x1t_l = sbuf("x1t_l", [P, CHUNKS, NODES], f32r)
        y_h = sbuf("y_h", [P, CHUNKS, NODES], f32r)
        y_l = sbuf("y_l", [P, CHUNKS, NODES], f32r)
        v_h = sbuf("v_h", [P, BLOCKS, VCOLS], f32r)
        v_l = sbuf("v_l", [P, BLOCKS, VCOLS], f32r)
        c_key = sbuf("c_key", [P, BLOCKS])
        expo = sbuf("expo", [P, BLOCKS, NODES])
        wgt = sbuf("wgt", [P, BLOCKS, NODES])
        wgt_h = sbuf("wgt_h", [P, BLOCKS, NODES], f32r)
        wgt_l = sbuf("wgt_l", [P, BLOCKS, NODES], f32r)
        u = sbuf("u", [P, BLOCKS, FEATURES])
        yout = sbuf("yout", [P, 2, BLOCKS, FEATURES])
        xmax = sbuf("xmax", [P, BLOCKS])
        mask = sbuf("mask", [P, BLOCKS])
        neg_half = sbuf("neg_half", [P, BLOCKS])
        stats1 = sbuf("stats1", [P, BLOCKS, 6])
        mv1 = sbuf("mv1", [P, BLOCKS, 2])
        var1 = sbuf("var1", [P, BLOCKS])
        rstd1 = sbuf("rstd1", [P, BLOCKS])
        mrstd1 = sbuf("mrstd1", [P, BLOCKS])
        shift1 = sbuf("shift1", [P, BLOCKS])
        rsum = sbuf("rsum", [P, BLOCKS])
        stats2 = sbuf("stats2", [P, BLOCKS, 6])
        mv2 = sbuf("mv2", [P, BLOCKS, 2])
        var2 = sbuf("var2", [P, BLOCKS])
        rstd2 = sbuf("rstd2", [P, BLOCKS])
        shift2 = sbuf("shift2", [P, BLOCKS])
        ident = sbuf("ident", [P, P])
        w0_f = sbuf("w0_f", [P, CHUNKS, FEATURES])
        w0_h = sbuf("w0_h", [P, CHUNKS, FEATURES], f32r)
        w0_l = sbuf("w0_l", [P, CHUNKS, FEATURES], f32r)
        wq_f = sbuf("wq_f", [P, CHUNKS, VCOLS])
        wk_f = sbuf("wk_f", [P, CHUNKS, FEATURES])
        wv_f = sbuf("wv_f", [P, CHUNKS, VCOLS])
        wv_h = sbuf("wv_h", [P, CHUNKS, VCOLS], f32r)
        wv_l = sbuf("wv_l", [P, CHUNKS, VCOLS], f32r)
        wqk_h = sbuf("wqk_h", [P, CHUNKS, FEATURES], f32r)
        wqk_l = sbuf("wqk_l", [P, CHUNKS, FEATURES], f32r)
        bqr = sbuf("bqr", [P, CHUNKS, P])
        bkc = sbuf("bkc", [P, CHUNKS])
        bv = sbuf("bv", [P, FEATURES])
        y_bias = sbuf("y_bias", [P, CHUNKS])
        bqbk = sbuf("bqbk", [P, 1])

        psum = ctx.enter_context(nc.psum_tensor("psum", [P, 8, BANK], f32))
        Y_BANK = [0, 1]
        V_BANK = 2
        S_BANK = [6, 7, 0, 1]
        T_BANK = [2, 3]
        O_BANK = [4, 5]
        X1T_BANK = [4, 5]
        Q_BANK = [6, 7, 3, 2]
        FOLD_BANK = [0, 1]
        BIAS_BANK = 6

        x_in = [sem("x_in0"), sem("x_in1")]
        adj_in = [sem("adj_in0"), sem("adj_in1")]
        adj0_in = [sem(f"adj0_in{k}") for k in range(BLOCKS)]
        stored = [sem("stored0"), sem("stored1")]
        last_stored = [sem("last_stored0"), sem("last_stored1")]
        w0_in, wk_in, wq_in, wv_in, bv_in, id_in = (
            sem(n) for n in ("w0_in", "wk_in", "wq_in", "wv_in", "bv_in", "id_in"))
        bk_in, bqr_in = sem("bk_in"), sem("bqr_in")
        const_set, w0h_out, w0l_out = sem("const_set"), sem("w0h_out"), sem("w0l_out")
        fold_mm, bias_mm, bias_out = sem("fold_mm"), sem("bias_mm"), sem("bias_out")
        wqkh_out, wqkl_out = sem("wqkh_out"), sem("wqkl_out")
        wvc_out, wvh_out, wvl_out = sem("wvc_out"), sem("wvh_out"), sem("wvl_out")
        xh_out, xl_out = sem("xh_out"), sem("xl_out")
        adjh_out, adjl_out = sem("adjh_out"), sem("adjl_out")
        t_mm, th_out, tl_out = sem("t_mm"), sem("th_out"), sem("tl_out")
        o_mm, r_out = sem("o_mm"), sem("r_out")
        mask_max, mask_out = sem("mask_max"), sem("mask_out")
        mv1_out, var1_out = sem("mv1_out"), sem("var1_out")
        rstd1_out, mrstd1_out = sem("rstd1_out"), sem("mrstd1_out")
        shift1_out, x1_out, x1_out_act = sem("shift1_out"), sem("x1_out"), sem("x1_out_act")
        x1b_out = sem("x1b_out")
        x1t_mm, x1th_out, x1tl_out = sem("x1t_mm"), sem("x1th_out"), sem("x1tl_out")
        y_mm, yh_out, yl_out = sem("y_mm"), sem("yh_out"), sem("yl_out")
        v_mm, vh_out, vl_out = sem("v_mm"), sem("vh_out"), sem("vl_out")
        c_out = sem("c_out")
        s_mm, exp_out = sem("s_mm"), sem("exp_out")
        wgt_out, wgth_out, wgtl_out = sem("wgt_out"), sem("wgth_out"), sem("wgtl_out")
        q_mm, rsum_out, u_out = sem("q_mm"), sem("rsum_out"), sem("u_out")
        mv2_out, var2_out, rstd2_out, shift2_out = sem("mv2_out"), sem("var2_out"), sem("rstd2_out"), sem("shift2_out")
        norm_out = sem("norm_out")

        def reach(engine, semaphore, i, m, each, nth):
            value = m * each + nth
            if isinstance(i, int):
                if i * each + value > 0:
                    engine.wait_ge(semaphore, i * each + value)
            else:
                engine.wait_ge(semaphore, i * each + value)

        def reach_dma(engine, by_parity, i, m, earlier=0):
            value = 16 * (m // 2 + 1 - earlier)
            if isinstance(i, int):
                if 8 * i + value > 0:
                    engine.wait_ge(by_parity[m % 2], 8 * i + value)
            else:
                engine.wait_ge(by_parity[m % 2], i * 8 + value)

        def exists(i, m):
            return not isinstance(i, int) or 0 <= i + m < GRAPHS

        def is_first(i, m):
            return isinstance(i, int) and i + m == 0

        def is_last(i, m):
            return isinstance(i, int) and i + m == GRAPHS - 1

        def each_turn(engine, turn):
            for b in range(-1, 2):
                turn(0, b)
            with engine.Fori(1, GRAPHS // 2 - 1) as pair:
                for m in range(2):
                    turn(pair * 2, m)
            for b in range(GRAPHS - 2, GRAPHS + 1):
                turn(0, b)

        def graph(dram, i, m):
            return dram[bass.ds(i + m, 1), :, :].rearrange("g p n -> (g p) n")

        def passes(high, low, moving_high, moving_low):
            return ((high, moving_high), (high, moving_low), (low, moving_high))

        def low_last(high, low, moving_high, moving_low):
            return ([(high, mv, c) for c in range(CHUNKS) for mv in (moving_high, moving_low)]
                    + [(low, moving_high, c) for c in range(CHUNKS)])

        block = ctx.enter_context(nc.Block())

        @block.sync
        def _(sp):
            def load_x(i, m):
                sp.dma_start(xin[:, m % 2].rearrange("p k f -> p (k f)"), graph(x, i, m)).then_inc(x_in[m % 2], 16)

            def store_pair(pair):
                cols = slice(2 * pair * FEATURES, 2 * (pair + 1) * FEATURES)
                sp.dma_start(out[GRAPHS - 1, :, cols],
                             yout[:, (GRAPHS - 1) % 2, 2 * pair:2 * pair + 2, :].rearrange("p k f -> p (k f)")
                             ).then_inc(last_stored[pair], 16)

            def load_adj(i, m):
                sp.dma_start(adj[:, m % 2].rearrange("p k n -> p (k n)"), graph(adj_t, i, m)).then_inc(adj_in[m % 2], 16)

            load_x(0, 0)
            for k in range(BLOCKS):
                sp.dma_start(adj[:, 0, k, :], adj_t[0, :, k * NODES:(k + 1) * NODES]).then_inc(adj0_in[k], 16)
            for tile, dram, loaded in ((w0_f, w0, w0_in), (wk_f, wk, wk_in), (wq_f, wq_bq, wq_in), (wv_f, wv_t, wv_in)):
                sp.dma_start(tile[:, :, :].rearrange("p k f -> p (k f)"), dram).then_inc(loaded, 16)
            sp.dma_start(ident[:, :], identity).then_inc(id_in, 16)
            sp.dma_start(bkc[:, :], bk_col).then_inc(bk_in, 16)
            sp.dma_start(bqr[:, :, :].rearrange("p k f -> p (k f)"), bq_rep).then_inc(bqr_in, 16)
            sp.dma_start(bv[:, :], bv_rep).then_inc(bv_in, 16)
            load_x(0, 1)
            load_adj(0, 1)

            def turn(i, m):
                if exists(i, m) and exists(i, m + 2):
                    reach(sp, r_out, i, m, 2, 2)
                    load_x(i, m + 2)
                if exists(i, m - 1):
                    if is_last(i, m - 1):
                        sp.wait_ge(norm_out, 2 * GRAPHS)
                        store_pair(1)
                    else:
                        reach(sp, norm_out, i, m - 1, 2, 2)
                        sp.dma_start(graph(out, i, m - 1), yout[:, (m - 1) % 2].rearrange("p k f -> p (k f)")
                                     ).then_inc(stored[(m - 1) % 2], 16)
                if exists(i, m) and exists(i, m + 2):
                    reach(sp, wgt_out, i, m, 4, 4)
                    load_adj(i, m + 2)
                if is_last(i, m):
                    sp.wait_ge(norm_out, 2 * GRAPHS - 1)
                    store_pair(0)

            each_turn(sp, turn)
            sp.wait_ge(stored[0], 16 * GRAPHS // 2)
            sp.wait_ge(stored[1], 16 * (GRAPHS // 2 - 1))
            for pair in range(2):
                sp.wait_ge(last_stored[pair], 16)

        @block.tensor
        def _(pe):
            def fold_weights():
                pe.wait_ge(wk_in, 16)
                pe.wait_ge(wq_in, 16)
                for c in range(CHUNKS):
                    for o in range(CHUNKS):
                        last = nc.tensor.matmul(psum[:, FOLD_BANK[c], 0:VCOLS], wk_f[:, o, c * P:(c + 1) * P],
                                                wq_f[:, o, :], start=(o == 0), stop=(o == CHUNKS - 1))
                last.then_inc(fold_mm, 1)

            def fold_biases():
                pe.wait_ge(bk_in, 16)
                pe.wait_ge(bqr_in, 16)
                for c in range(CHUNKS):
                    for o in range(CHUNKS):
                        nc.tensor.matmul(psum[:, BIAS_BANK, c:c + 1], wq_f[:, o, c * P:(c + 1) * P], bkc[:, o:o + 1],
                                         start=(o == 0), stop=(o == CHUNKS - 1))
                for o in range(CHUNKS):
                    last = nc.tensor.matmul(psum[:, BIAS_BANK, CHUNKS:CHUNKS + 1], bqr[:, o, :], bkc[:, o:o + 1],
                                            start=(o == 0), stop=(o == CHUNKS - 1))
                last.then_inc(bias_mm, 1)

            def make_y(i, m):
                order = ([(w, x1t_h, c) for c in range(CHUNKS) for w in (wqk_h, wqk_l)]
                         + [(wqk_h, x1t_l, c) for c in range(CHUNKS)])
                for fo in range(CHUNKS):
                    for n, (w, mv, c) in enumerate(order):
                        if fo == 0 and n % 2 == 0 and n < 2 * CHUNKS:
                            reach(pe, x1th_out, i, m, 2, c + 1)
                        if fo == 0 and n >= 2 * CHUNKS:
                            reach(pe, x1tl_out, i, m, 2, c + 1)
                        last = nc.tensor.matmul(psum[:, Y_BANK[fo], :], w[:, c, fo * P:(fo + 1) * P], mv[:, c, :],
                                                start=(n == 0), stop=(n == len(order) - 1))
                    last.then_inc(y_mm, 1)

            def make_v(i, m):
                reach(pe, u_out, i, m - 1, 4, 4)
                for k in range(BLOCKS):
                    rows = slice(k * P, (k + 1) * P)
                    for n, (st, mv, c) in enumerate(low_last(x1t_h, x1t_l, wv_h, wv_l)):
                        last = nc.tensor.matmul(psum[:, V_BANK + k, 0:VCOLS], st[:, c, rows], mv[:, c, :],
                                                start=(n == 0), stop=(n == 3 * CHUNKS - 1))
                    if k % 2:
                        last.then_inc(v_mm, 1)

            def make_scores(i, m):
                reach(pe, yh_out, i, m, 2, 2)
                reach(pe, yl_out, i, m, 2, 2)
                for k in range(BLOCKS):
                    rows = slice(k * P, (k + 1) * P)
                    for n, (st, mv, c) in enumerate(low_last(y_h, y_l, x1t_h, x1t_l)):
                        last = nc.tensor.matmul(psum[:, S_BANK[k], :], st[:, c, rows], mv[:, c, :],
                                                start=(n == 0), stop=(n == 3 * CHUNKS - 1))
                    last.then_inc(s_mm, 1)

            def make_t(i, m):
                reach(pe, xh_out, i, m, 1, 1)
                reach(pe, xl_out, i, m, 1, 1)
                reach(pe, vl_out, i, m - 1, 2, 2)
                for half in range(2):
                    nodes = slice(half * HALF, (half + 1) * HALF)
                    for f in range(CHUNKS):
                        cols = slice(f * P, (f + 1) * P)
                        for k in range(BLOCKS):
                            if half == 0 and f == 0:
                                reach(pe, adjh_out, i, m, 4, k + 1)
                                reach(pe, adjl_out, i, m, 4, k + 1)
                            for n, (st, mv) in enumerate(passes(x_h, x_l, adj_h, adj_l)):
                                last = nc.tensor.matmul(psum[:, T_BANK[half], f * HALF:(f + 1) * HALF],
                                                        st[:, k, cols], mv[:, k, nodes],
                                                        start=(k == 0 and n == 0), stop=(k == BLOCKS - 1 and n == 2))
                    last.then_inc(t_mm, 1)

            def make_o(i, m):
                for half in range(2):
                    reach(pe, th_out, i, m, 2, half + 1)
                    for k in range(2):
                        rows = slice(k * P, (k + 1) * P)
                        for n, (st, mv, c) in enumerate(low_last(t_h, t_l, w0_h, w0_l)):
                            if k == 0 and n == 2 * CHUNKS:
                                reach(pe, tl_out, i, m, 2, half + 1)
                            last = nc.tensor.matmul(psum[:, O_BANK[half], k * FEATURES:(k + 1) * FEATURES],
                                                    st[:, half, c, rows], mv[:, c, :],
                                                    start=(n == 0), stop=(n == 3 * CHUNKS - 1))
                    last.then_inc(o_mm, 1)

            def make_attention(i, m, q):
                if q == 0:
                    reach(pe, vh_out, i, m, 2, 2)
                    reach(pe, vl_out, i, m, 2, 2)
                rows = slice(q * P, (q + 1) * P)
                for k in range(BLOCKS):
                    if q == 0:
                        reach(pe, wgth_out, i, m, 4, k + 1)
                        reach(pe, wgtl_out, i, m, 4, k + 1)
                    for n, (st, mv) in enumerate(passes(wgt_h, wgt_l, v_h, v_l)):
                        last = nc.tensor.matmul(psum[:, Q_BANK[q], 0:VCOLS], st[:, k, rows], mv[:, k, :],
                                                start=(k == 0 and n == 0), stop=(k == BLOCKS - 1 and n == 2))
                last.then_inc(q_mm, 1)

            def make_x1t(i, m):
                for k in range(BLOCKS):
                    if k % 2 == 0:
                        reach(pe, x1_out, i, m, 2, k // 2 + 1)
                    else:
                        reach(pe, x1_out_act, i, m, 2, k // 2 + 1)
                    for c in range(CHUNKS):
                        last = nc.tensor.transpose(psum[:, X1T_BANK[c], k * P:(k + 1) * P],
                                                   x1[:, k, c * P:(c + 1) * P], ident[:, :])
                last.then_inc(x1t_mm, 1)

            def turn(i, m):
                if exists(i, m):
                    if is_first(i, m):
                        pe.wait_ge(wqkh_out, 1)
                        pe.wait_ge(wqkl_out, 1)
                    make_y(i, m)
                    if is_first(i, m):
                        pe.wait_ge(wvh_out, 1)
                        pe.wait_ge(wvl_out, 1)
                    make_v(i, m)
                    make_scores(i, m)
                if exists(i, m + 1):
                    make_t(i, m + 1)
                    if is_first(i, m + 1):
                        pe.wait_ge(w0h_out, 1)
                        pe.wait_ge(w0l_out, 1)
                    make_o(i, m + 1)
                    if is_first(i, m + 1):
                        fold_weights()
                if exists(i, m):
                    for q in range(3):
                        make_attention(i, m, q)
                if exists(i, m + 1):
                    if is_first(i, m + 1):
                        pe.wait_ge(id_in, 16)
                    make_x1t(i, m + 1)
                    if is_first(i, m + 1):
                        fold_biases()
                if exists(i, m):
                    make_attention(i, m, 3)

            each_turn(pe, turn)

        @block.scalar
        def _(act):
            flat = lambda t: t[:, :, :].rearrange("p a b -> p (a b)")
            nc.scalar.preload_act_table(ACT.Exp)

            def split_x(i, m):
                reach_dma(act, x_in, i, m)
                nc.scalar.activation(flat(x_h), xin[:, m % 2].rearrange("p k f -> p (k f)"), ACT.Copy).then_inc(xh_out, 1)

            def split_adj(i, m, k):
                if is_first(i, m):
                    act.wait_ge(adj0_in[k], 16)
                elif k == 0:
                    reach_dma(act, adj_in, i, m, earlier=(m + 1) % 2)
                nc.scalar.activation(adj_h[:, k, :], adj[:, m % 2, k, :], ACT.Copy).then_inc(adjh_out, 1)

            split_x(0, 0)

            def normalise(i, m, pair):
                reach(act, shift2_out, i, m, 2, pair + 1)
                if pair == 0:
                    reach_dma(act, stored, i, m - 2)
                for k in (2 * pair, 2 * pair + 1):
                    last = nc.scalar.activation(yout[:, m % 2, k, :], u[:, k, :], ACT.Identity,
                                                bias=shift2[:, k:k + 1], scale=rstd2[:, k:k + 1])
                last.then_inc(norm_out, 1)

            def turn(i, m):
                now, after = exists(i, m), exists(i, m + 1)
                if after:
                    split_adj(i, m + 1, 0)
                    split_adj(i, m + 1, 1)
                for fo in range(CHUNKS):
                    if now:
                        if is_first(i, m) and fo == 0:
                            act.wait_ge(bias_out, 1)
                        reach(act, y_mm, i, m, 2, fo + 1)
                        nc.scalar.activation(y_h[:, fo, :], psum[:, Y_BANK[fo], :], ACT.Identity,
                                             bias=y_bias[:, fo:fo + 1]).then_inc(yh_out, 1)
                    if after:
                        split_adj(i, m + 1, 2 + fo)
                if is_first(i, m + 1):
                    act.wait_ge(w0_in, 16)
                    nc.scalar.activation(flat(w0_h), flat(w0_f), ACT.Copy).then_inc(w0h_out, 1)
                if now:
                    for pair in range(2):
                        reach(act, v_mm, i, m, 2, pair + 1)
                        nc.scalar.activation(v_h[:, 2 * pair:2 * pair + 2, 0:FEATURES],
                                             psum[:, V_BANK + 2 * pair:V_BANK + 2 * pair + 2, 0:FEATURES],
                                             ACT.Copy).then_inc(vh_out, 1)
                if exists(i, m - 1) and not is_last(i, m):
                    if not is_last(i, m - 1):
                        normalise(i, m - 1, 0)
                    normalise(i, m - 1, 1)

                def split_weights(k):
                    reach(act, wgt_out, i, m, 4, k + 1)
                    nc.scalar.activation(wgt_h[:, k, :], wgt[:, k, :], ACT.Copy).then_inc(wgth_out, 1)

                if now:
                    reach(act, c_out, i, m, 1, 1)
                    for k in range(BLOCKS):
                        reach(act, s_mm, i, m, 4, k + 1)
                        nc.scalar.activation(expo[:, k, :], psum[:, S_BANK[k], :], ACT.Exp,
                                             bias=c_key[:, k:k + 1]).then_inc(exp_out, 1)
                        if k:
                            split_weights(k - 1)
                    split_weights(BLOCKS - 1)
                if after:
                    for half in range(2):
                        reach(act, t_mm, i, m + 1, 2, half + 1)
                        nc.scalar.activation(t_h[:, half].rearrange("p c n -> p (c n)"), psum[:, T_BANK[half], :],
                                             ACT.Copy).then_inc(th_out, 1)
                if exists(i, m + 2) and exists(i, m + 1):
                    split_x(i, m + 2)
                if after:
                    for half in range(2):
                        k = 2 * half + 1
                        reach(act, shift1_out, i, m + 1, 2, half + 1)
                        nc.scalar.activation(x1[:, k, :], r[:, k, :], ACT.Identity, bias=shift1[:, k:k + 1],
                                             scale=mrstd1[:, k:k + 1]).then_inc(x1_out_act, 1)
                if is_first(i, m + 1):
                    act.wait_ge(fold_mm, 1)
                    nc.scalar.activation(wqk_h[:, :, :], psum[:, 0:2, 0:FEATURES], ACT.Copy).then_inc(wqkh_out, 1)
                    act.wait_ge(wvc_out, 1)
                    nc.scalar.activation(flat(wv_h), flat(wv_f), ACT.Copy).then_inc(wvh_out, 1)
                if after:
                    reach(act, x1t_mm, i, m + 1, 1, 1)
                    for c in range(CHUNKS):
                        nc.scalar.activation(x1t_h[:, c, :], psum[:, X1T_BANK[c], :], ACT.Copy).then_inc(x1th_out, 1)
                if is_last(i, m):
                    normalise(i, m - 1, 0)
                    normalise(i, m - 1, 1)
                    normalise(i, m, 0)

            each_turn(act, turn)

        @block.vector
        def _(dve):
            flat = lambda t: t[:, :, :].rearrange("p a b -> p (a b)")
            as32 = lambda ap: ap.bitcast(f32)

            nc.vector.memset(neg_half[:, :], -0.5).then_inc(const_set, 1)
            nc.vector.memset(as32(v_h[:, :, FEATURES:FEATURES + 1]), 1.0)
            nc.vector.memset(as32(v_h[:, :, FEATURES + 1:VCOLS]), 0.0)
            nc.vector.memset(as32(v_l[:, :, FEATURES:VCOLS]), 0.0)

            def find_mask(i, m):
                reach_dma(dve, x_in, i, m)
                nc.vector.tensor_reduce(xmax[:, :], xin[:, m % 2], AX.X, ALU.max,
                                        apply_absolute_value=True).then_inc(mask_max, 1)
                reach(dve, mask_max, i, m, 1, 1)
                nc.vector.tensor_scalar(mask[:, :], xmax[:, :], 0.0, None, ALU.is_gt).then_inc(mask_out, 1)

            def add_attention(i, m, queries):
                for q in queries:
                    reach(dve, q_mm, i, m, 4, q + 1)
                    nc.vector.reciprocal(rsum[:, q:q + 1], psum[:, Q_BANK[q], FEATURES:FEATURES + 1]).then_inc(rsum_out, 1)
                if queries[0] == 0:
                    reach(dve, x1b_out, i, m, 1, 1)
                for q in queries:
                    reach(dve, rsum_out, i, m, 4, q + 1)
                    nc.vector.scalar_tensor_tensor(u[:, q, :], psum[:, Q_BANK[q], 0:FEATURES], rsum[:, q:q + 1],
                                                   x1b[:, q, :], ALU.mult, ALU.add).then_inc(u_out, 1)

            def sum_statistics(i, m, queries):
                for q in queries:
                    reach(dve, u_out, i, m, 4, q + 1)
                    nc.vector.bn_stats(stats2[:, q, :], u[:, q, :])

            def find_variances(i, m, pairs):
                dve.drain()
                for pair in pairs:
                    for q in (2 * pair, 2 * pair + 1):
                        last = nc.vector.bn_aggr(mv2[:, q, :], stats2[:, q, :])
                    last.then_inc(mv2_out, 1)
                for pair in pairs:
                    blocks = slice(2 * pair, 2 * pair + 2)
                    reach(dve, mv2_out, i, m, 2, pair + 1)
                    nc.vector.tensor_scalar(var2[:, blocks], mv2[:, blocks, 1], EPS, None, ALU.add).then_inc(var2_out, 1)

            def find_shift(i, m, pair):
                blocks = slice(2 * pair, 2 * pair + 2)
                reach(dve, rstd2_out, i, m, 2, pair + 1)
                nc.vector.scalar_tensor_tensor(shift2[:, blocks], mv2[:, blocks, 0], -1.0, rstd2[:, blocks],
                                               ALU.mult, ALU.mult).then_inc(shift2_out, 1)

            def turn(i, m):
                now, after = exists(i, m), exists(i, m + 1)
                if exists(i, m - 1):
                    if is_last(i, m - 1):
                        for q in (2, 3):
                            add_attention(i, m - 1, (q,))
                            sum_statistics(i, m - 1, (q,))
                        find_variances(i, m - 1, (1,))
                        find_shift(i, m - 1, 1)
                    else:
                        add_attention(i, m - 1, (2, 3))
                        sum_statistics(i, m - 1, (0, 1))
                if is_first(i, m + 1):
                    for k in range(BLOCKS):
                        dve.wait_ge(adjh_out, k + 1)
                        nc.vector.tensor_tensor(adj_l[:, k, :], adj[:, 0, k, :], as32(adj_h[:, k, :]),
                                                ALU.subtract).then_inc(adjl_out, 1)
                for fo in range(CHUNKS):
                    if now:
                        reach(dve, yh_out, i, m, 2, fo + 1)
                        nc.vector.scalar_tensor_tensor(y_l[:, fo, :], psum[:, Y_BANK[fo], :], y_bias[:, fo:fo + 1],
                                                       as32(y_h[:, fo, :]), ALU.add, ALU.subtract).then_inc(yl_out, 1)
                    if exists(i, m - 1) and not is_last(i, m - 1):
                        if fo == 0:
                            sum_statistics(i, m - 1, (2, 3))
                            find_variances(i, m - 1, (0, 1))
                        else:
                            find_shift(i, m - 1, 0)
                            find_shift(i, m - 1, 1)
                if now:
                    for pair in range(2):
                        reach(dve, vh_out, i, m, 2, pair + 1)
                        if pair == 1:
                            nc.vector.tensor_scalar(c_key[:, :], psum[:, V_BANK:V_BANK + BLOCKS, FEATURES],
                                                    bqbk[:, 0:1], None, ALU.add).then_inc(c_out, 1)
                        nc.vector.tensor_tensor(v_l[:, 2 * pair:2 * pair + 2, 0:FEATURES],
                                                psum[:, V_BANK + 2 * pair:V_BANK + 2 * pair + 2, 0:FEATURES],
                                                as32(v_h[:, 2 * pair:2 * pair + 2, 0:FEATURES]),
                                                ALU.subtract).then_inc(vl_out, 1)
                if after:
                    find_mask(i, m + 1)

                def split_weights(k):
                    reach(dve, wgth_out, i, m, 4, k + 1)
                    nc.vector.tensor_tensor(wgt_l[:, k, :], wgt[:, k, :], as32(wgt_h[:, k, :]),
                                            ALU.subtract).then_inc(wgtl_out, 1)

                if now:
                    for k in range(BLOCKS):
                        reach(dve, exp_out, i, m, 4, k + 1)
                        nc.vector.tensor_tensor(wgt[:, k, :], expo[:, k, :], adj[:, m % 2, k, :],
                                                ALU.mult).then_inc(wgt_out, 1)
                        if k:
                            split_weights(k - 1)
                    split_weights(BLOCKS - 1)
                if after:
                    for half in range(2):
                        reach(dve, th_out, i, m + 1, 2, half + 1)
                        nc.vector.tensor_tensor(t_l[:, half].rearrange("p c n -> p (c n)"), psum[:, T_BANK[half], :],
                                                as32(t_h[:, half].rearrange("p c n -> p (c n)")),
                                                ALU.subtract).then_inc(tl_out, 1)
                    for half in range(2):
                        blocks = slice(2 * half, 2 * half + 2)
                        reach(dve, o_mm, i, m + 1, 2, half + 1)
                        nc.vector.scalar_tensor_tensor(r[:, blocks, :].rearrange("p k f -> p (k f)"),
                                                       psum[:, O_BANK[half], :], 0.0,
                                                       xin[:, (m + 1) % 2, blocks, :].rearrange("p k f -> p (k f)"),
                                                       ALU.max, ALU.add).then_inc(r_out, 1)
                        reach(dve, r_out, i, m + 1, 2, half + 1)
                        for k in (2 * half, 2 * half + 1):
                            nc.vector.bn_stats(stats1[:, k, :], r[:, k, :])
                        dve.drain()
                        for k in (2 * half, 2 * half + 1):
                            last = nc.vector.bn_aggr(mv1[:, k, :], stats1[:, k, :])
                        last.then_inc(mv1_out, 1)
                        reach(dve, mv1_out, i, m + 1, 2, half + 1)
                        nc.vector.tensor_scalar(var1[:, blocks], mv1[:, blocks, 1], EPS, None, ALU.add).then_inc(var1_out, 1)
                    reach(dve, mask_out, i, m + 1, 1, 1)
                    reach(dve, x1b_out, i, m, 1, 1)
                    for half in range(2):
                        blocks = slice(2 * half, 2 * half + 2)
                        reach(dve, rstd1_out, i, m + 1, 2, half + 1)
                        nc.vector.tensor_tensor(mrstd1[:, blocks], rstd1[:, blocks], mask[:, blocks],
                                                ALU.mult).then_inc(mrstd1_out, 1)
                        reach(dve, mrstd1_out, i, m + 1, 2, half + 1)
                        k = 2 * half
                        nc.vector.scalar_tensor_tensor(shift1[:, k + 1:k + 2], mv1[:, k + 1, 0:1], -1.0,
                                                       mrstd1[:, k + 1:k + 2], ALU.mult, ALU.mult).then_inc(shift1_out, 1)
                        nc.vector.tensor_scalar(x1[:, k, :], r[:, k, :], mv1[:, k, 0:1], mrstd1[:, k:k + 1],
                                                ALU.subtract, ALU.mult).then_inc(x1_out, 1)
                if is_last(i, m):
                    dve.wait_ge(norm_out, 2 * (GRAPHS - 1))
                if now:
                    add_attention(i, m, (0, 1))
                if is_first(i, m + 1):
                    dve.wait_ge(wqkh_out, 1)
                    nc.vector.tensor_tensor(wqk_l[:, :, :], psum[:, 0:2, 0:FEATURES], as32(wqk_h[:, :, :]),
                                            ALU.subtract).then_inc(wqkl_out, 1)
                    dve.wait_ge(wv_in, 16)
                    nc.vector.tensor_copy(wv_f[:, :, FEATURES], psum[:, 0:2, FEATURES]).then_inc(wvc_out, 1)
                if after:
                    for c in range(CHUNKS):
                        reach(dve, x1th_out, i, m + 1, 2, c + 1)
                        nc.vector.tensor_tensor(x1t_l[:, c, :], psum[:, X1T_BANK[c], :], as32(x1t_h[:, c, :]),
                                                ALU.subtract).then_inc(x1tl_out, 1)
                if is_last(i, m):
                    sum_statistics(i, m, (0, 1))
                    find_variances(i, m, (0,))
                    find_shift(i, m, 0)
                if is_first(i, m + 1):
                    dve.wait_ge(bias_mm, 1)
                    nc.vector.tensor_copy(bqbk[:, :], psum[:, BIAS_BANK, CHUNKS:CHUNKS + 1])
                    nc.vector.tensor_copy(y_bias[:, :], psum[:, BIAS_BANK, 0:CHUNKS]).then_inc(bias_out, 1)

            each_turn(dve, turn)

        @block.gpsimd
        def _(pool):
            flat = lambda t: t[:, :, :].rearrange("p a b -> p (a b)")
            as32 = lambda ap: ap.bitcast(f32)

            def split_x(i, m):
                reach(pool, xh_out, i, m, 1, 1)
                nc.gpsimd.tensor_tensor(flat(x_l), xin[:, m % 2].rearrange("p k f -> p (k f)"), as32(flat(x_h)),
                                        ALU.subtract).then_inc(xl_out, 1)

            def find_deviation(i, m, pair):
                blocks = slice(2 * pair, 2 * pair + 2)
                reach(pool, var2_out, i, m, 2, pair + 1)
                nc.gpsimd.tensor_tensor(rstd2[:, blocks], var2[:, blocks], neg_half[:, blocks],
                                        ALU.pow).then_inc(rstd2_out, 1)

            split_x(0, 0)
            pool.wait_ge(w0h_out, 1)
            nc.gpsimd.tensor_tensor(flat(w0_l), flat(w0_f), as32(flat(w0_h)), ALU.subtract).then_inc(w0l_out, 1)
            pool.wait_ge(const_set, 1)

            def turn(i, m):
                if exists(i, m - 1):
                    if not is_last(i, m - 1):
                        find_deviation(i, m - 1, 0)
                    find_deviation(i, m - 1, 1)
                if exists(i, m + 1) and not is_first(i, m + 1):
                    for k in range(BLOCKS):
                        reach(pool, adjh_out, i, m + 1, 4, k + 1)
                        nc.gpsimd.tensor_tensor(adj_l[:, k, :], adj[:, (m + 1) % 2, k, :], as32(adj_h[:, k, :]),
                                                ALU.subtract).then_inc(adjl_out, 1)
                if exists(i, m):
                    if is_first(i, m):
                        pool.wait_ge(bv_in, 16)
                    reach(pool, x1_out, i, m, 2, 2)
                    reach(pool, x1_out_act, i, m, 2, 2)
                    nc.gpsimd.tensor_tensor(x1b[:, :, :], x1[:, :, :],
                                            bv[:, :].unsqueeze(1).to_broadcast([P, BLOCKS, FEATURES]),
                                            ALU.add).then_inc(x1b_out, 1)
                if exists(i, m + 1):
                    for half in range(2):
                        blocks = slice(2 * half, 2 * half + 2)
                        reach(pool, var1_out, i, m + 1, 2, half + 1)
                        nc.gpsimd.tensor_tensor(rstd1[:, blocks], var1[:, blocks], neg_half[:, blocks],
                                                ALU.pow).then_inc(rstd1_out, 1)
                if is_first(i, m + 1):
                    pool.wait_ge(wvh_out, 1)
                    nc.gpsimd.tensor_tensor(flat(wv_l), flat(wv_f), as32(flat(wv_h)), ALU.subtract).then_inc(wvl_out, 1)
                if exists(i, m + 2) and exists(i, m + 1):
                    split_x(i, m + 2)
                if is_last(i, m):
                    find_deviation(i, m, 0)

            each_turn(pool, turn)


def kernel(x, adj, L0_gnn_kernel, L1_gnn_Wq_w, L1_gnn_Wq_b, L1_gnn_Wk_w, L1_gnn_Wk_b, L1_gnn_Wv_w, L1_gnn_Wv_b):
    import numpy as np
    import concourse.bacc as bacc
    from concourse import mybir as mb
    from concourse.bass_utils import run_bass_kernel_spmd

    def by_partition(a):
        a = np.asarray(a)
        *lead, rows, n = a.shape
        a = a.reshape(*lead, rows // P, P, n)
        return np.ascontiguousarray(np.moveaxis(a, -3, -2).reshape(*lead, P, rows // P * n))

    wv_t = np.asarray(L1_gnn_Wv_w).T
    wv_t = np.concatenate([wv_t, np.zeros((FEATURES, VCOLS - FEATURES), wv_t.dtype)], axis=1)
    bq = np.asarray(L1_gnn_Wq_b)[:, None]
    wq_bq = np.concatenate([np.asarray(L1_gnn_Wq_w), bq, np.zeros_like(bq)], axis=1)
    ins = {
        "x": by_partition(x),
        "adj_t": by_partition(np.swapaxes(np.asarray(adj), 1, 2)),
        "w0": by_partition(L0_gnn_kernel),
        "wq_bq": by_partition(wq_bq),
        "wk": by_partition(L1_gnn_Wk_w),
        "wv_t": by_partition(wv_t),
        "bq_rep": by_partition(np.repeat(bq, P, axis=1)),
        "bk_col": by_partition(np.asarray(L1_gnn_Wk_b)[:, None]),
        "bv_rep": np.ascontiguousarray(np.repeat(np.asarray(L1_gnn_Wv_b)[None, :], P, axis=0)),
        "identity": np.eye(P, dtype=np.float32),
    }
    nc = bacc.Bacc("TRN2", target_bir_lowering=False, num_devices=1)
    args = [nc.dram_tensor(f"in_{n}", a.shape, mb.dt.from_np(a.dtype), kind="ExternalInput").ap() for n, a in ins.items()]
    out = nc.dram_tensor("out", (GRAPHS, P, BLOCKS * FEATURES), mb.dt.float32, kind="ExternalOutput").ap()
    build(nc, *args, out)
    got = run_bass_kernel_spmd(nc, [{f"in_{n}": a for n, a in ins.items()}], core_ids=[0]).results[0]["out"]
    return np.ascontiguousarray(
        got.reshape(GRAPHS, P, BLOCKS, FEATURES).transpose(0, 2, 1, 3).reshape(GRAPHS, NODES, FEATURES))
```

```python
import concourse.bass as bass
from concourse import mybir
from contextlib import ExitStack

P = 128
GRAPHS = 16
NODES = 512
FEATURES = 256
BLOCKS = NODES // P
CHUNKS = FEATURES // P
HALF = NODES // 2
VCOLS = FEATURES + 2
BANK = 512
EPS = 1e-5
COPIES = 64


def build(nc, x, adj_t, w0, wq_bq, wk, wv_t, bq_rep, bk_rep, bv_rep, identity, out):
    f32, f32r = mybir.dt.float32, mybir.dt.float32r
    ALU, ACT, AX = mybir.AluOpType, mybir.ActivationFunctionType, mybir.AxisListType

    with ExitStack() as ctx:
        def sbuf(name, shape, dtype=f32):
            return ctx.enter_context(nc.sbuf_tensor(name, shape, dtype))

        def sem(name):
            return ctx.enter_context(nc.semaphore(name))

        adj = sbuf("adj", [P, 2, BLOCKS, NODES])
        xin = sbuf("xin", [P, 2, BLOCKS, FEATURES])
        adj_h = sbuf("adj_h", [P, BLOCKS, NODES], f32r)
        adj_l = sbuf("adj_l", [P, BLOCKS, NODES], f32r)
        x_h = sbuf("x_h", [P, 2, BLOCKS, FEATURES], f32r)
        x_l = sbuf("x_l", [P, 2, BLOCKS, FEATURES], f32r)
        warm = sbuf("warm", [P, HALF], f32r)
        t_h = sbuf("t_h", [P, 2, CHUNKS, HALF], f32r)
        t_l = sbuf("t_l", [P, 2, CHUNKS, HALF], f32r)
        r = sbuf("r", [P, BLOCKS, FEATURES])
        x1 = sbuf("x1", [P, BLOCKS, FEATURES])
        x1b = sbuf("x1b", [P, BLOCKS, FEATURES])
        x1t_h = sbuf("x1t_h", [P, CHUNKS, NODES], f32r)
        x1t_l = sbuf("x1t_l", [P, CHUNKS, NODES], f32r)
        y_h = sbuf("y_h", [P, CHUNKS, NODES], f32r)
        y_l = sbuf("y_l", [P, CHUNKS, NODES], f32r)
        v_h = sbuf("v_h", [P, BLOCKS, VCOLS], f32r)
        v_l = sbuf("v_l", [P, BLOCKS, VCOLS], f32r)
        c_key = sbuf("c_key", [P, BLOCKS])
        expo = sbuf("expo", [P, BLOCKS, NODES])
        wgt = sbuf("wgt", [P, BLOCKS, NODES])
        wgt_h = sbuf("wgt_h", [P, BLOCKS, NODES], f32r)
        wgt_l = sbuf("wgt_l", [P, BLOCKS, NODES], f32r)
        u = sbuf("u", [P, BLOCKS, FEATURES])
        yout = sbuf("yout", [P, 2, BLOCKS, FEATURES])
        xmax = sbuf("xmax", [P, BLOCKS])
        mask = sbuf("mask", [P, BLOCKS])
        neg_half = sbuf("neg_half", [P, BLOCKS])
        stats1 = sbuf("stats1", [P, BLOCKS, 6])
        mv1 = sbuf("mv1", [P, BLOCKS, 2])
        var1 = sbuf("var1", [P, BLOCKS])
        rstd1 = sbuf("rstd1", [P, BLOCKS])
        mrstd1 = sbuf("mrstd1", [P, BLOCKS])
        shift1 = sbuf("shift1", [P, BLOCKS])
        rsum = sbuf("rsum", [P, BLOCKS])
        stats2 = sbuf("stats2", [P, BLOCKS, 6])
        mv2 = sbuf("mv2", [P, BLOCKS, 2])
        var2 = sbuf("var2", [P, BLOCKS])
        rstd2 = sbuf("rstd2", [P, BLOCKS])
        shift2 = sbuf("shift2", [P, BLOCKS])
        ident = sbuf("ident", [P, P])
        w0_f = sbuf("w0_f", [P, CHUNKS, FEATURES])
        w0_h = sbuf("w0_h", [P, CHUNKS, FEATURES], f32r)
        w0_l = sbuf("w0_l", [P, CHUNKS, FEATURES], f32r)
        wq_f = sbuf("wq_f", [P, CHUNKS, VCOLS])
        wk_f = sbuf("wk_f", [P, CHUNKS, FEATURES])
        wv_f = sbuf("wv_f", [P, CHUNKS, VCOLS])
        wv_h = sbuf("wv_h", [P, CHUNKS, VCOLS], f32r)
        wv_l = sbuf("wv_l", [P, CHUNKS, VCOLS], f32r)
        wqk_h = sbuf("wqk_h", [P, CHUNKS, FEATURES], f32r)
        wqk_l = sbuf("wqk_l", [P, CHUNKS, FEATURES], f32r)
        bqr = sbuf("bqr", [P, CHUNKS, P])
        bkr = sbuf("bkr", [P, CHUNKS, COPIES])
        bv = sbuf("bv", [P, FEATURES])
        y_bias = sbuf("y_bias", [P, CHUNKS])
        bqbk = sbuf("bqbk", [P, 1])

        psum = ctx.enter_context(nc.psum_tensor("psum", [P, 8, BANK], f32))
        Y_BANK = [0, 1]
        V_BANK = 2
        S_BANK = [6, 7, 0, 1]
        T_BANK = [2, 3]
        T0_BANK = [[2, 3], [6, 7]]
        O_BANK = [4, 5]
        X1T_BANK = [4, 5]
        Q_BANK = [6, 7, 3, 2]
        FOLD_BANK = [0, 1]
        BIAS_BANK = 6
        WARM_BANK = 7

        x_in = [sem("x_in0"), sem("x_in1")]
        adj_in = [sem("adj_in0"), sem("adj_in1")]
        x0_in = [sem(f"x0_in{k}") for k in range(BLOCKS)]
        adj0_in = [sem(f"adj0_in{k}") for k in range(BLOCKS)]
        stored = [sem("stored0"), sem("stored1")]
        last_stored = [sem(f"last_stored{n}") for n in range(3)]
        w0_in, wk_in, wq_in, wv_in, bv_in, id_in = (
            sem(n) for n in ("w0_in", "wk_in", "wq_in", "wv_in", "bv_in", "id_in"))
        bk_in, bqr_in = sem("bk_in"), sem("bqr_in")
        warm_set, const_set, w0h_out, w0l_out = sem("warm_set"), sem("const_set"), sem("w0h_out"), sem("w0l_out")
        fold_mm, bias_mm, bias_out = sem("fold_mm"), sem("bias_mm"), sem("bias_out")
        wqkh_out, wqkl_out = sem("wqkh_out"), sem("wqkl_out")
        wvc_out, wvh_out, wvl_out = sem("wvc_out"), sem("wvh_out"), sem("wvl_out")
        x0h_out, x0l_out = sem("x0h_out"), sem("x0l_out")
        xh_out, xl_out = sem("xh_out"), sem("xl_out")
        adjh_out, adjl_out = sem("adjh_out"), sem("adjl_out")
        t_mm, th_out, tl_out = sem("t_mm"), sem("th_out"), sem("tl_out")
        o_mm, r_out = sem("o_mm"), sem("r_out")
        mask_max, mask_out = sem("mask_max"), sem("mask_out")
        mv1_out, var1_out = sem("mv1_out"), sem("var1_out")
        rstd1_out, mrstd1_out = sem("rstd1_out"), sem("mrstd1_out")
        shift1_out, x1_out, x1_out_act = sem("shift1_out"), sem("x1_out"), sem("x1_out_act")
        x1b_out = sem("x1b_out")
        x1t_mm, x1th_out, x1tl_out = sem("x1t_mm"), sem("x1th_out"), sem("x1tl_out")
        y_mm, yh_out, yl_out = sem("y_mm"), sem("yh_out"), sem("yl_out")
        v_mm, vh_out, vl_out = sem("v_mm"), sem("vh_out"), sem("vl_out")
        c_out = sem("c_out")
        s_mm, exp_out = sem("s_mm"), sem("exp_out")
        wgt_out, wgth_out, wgtl_out = sem("wgt_out"), sem("wgth_out"), sem("wgtl_out")
        q_mm, rsum_out, u_out = sem("q_mm"), sem("rsum_out"), sem("u_out")
        mv2_out, var2_out, rstd2_out, shift2_out = sem("mv2_out"), sem("var2_out"), sem("rstd2_out"), sem("shift2_out")
        norm_out, norm_out_dve = sem("norm_out"), sem("norm_out_dve")

        def reach(engine, semaphore, i, m, each, nth):
            value = m * each + nth
            if isinstance(i, int):
                if i * each + value > 0:
                    engine.wait_ge(semaphore, i * each + value)
            else:
                engine.wait_ge(semaphore, i * each + value)

        def reach_dma(engine, by_parity, i, m, earlier=0):
            value = 16 * (m // 2 + 1 - earlier)
            if isinstance(i, int):
                if 8 * i + value > 0:
                    engine.wait_ge(by_parity[m % 2], 8 * i + value)
            else:
                engine.wait_ge(by_parity[m % 2], i * 8 + value)

        def exists(i, m):
            return not isinstance(i, int) or 0 <= i + m < GRAPHS

        def is_first(i, m):
            return isinstance(i, int) and i + m == 0

        def is_last(i, m):
            return isinstance(i, int) and i + m == GRAPHS - 1

        def each_turn(engine, turn):
            for b in range(-1, 2):
                turn(0, b)
            with engine.Fori(1, GRAPHS // 2 - 1) as pair:
                for m in range(2):
                    turn(pair * 2, m)
            for b in range(GRAPHS - 2, GRAPHS + 1):
                turn(0, b)

        def graph(dram, i, m):
            return dram[bass.ds(i + m, 1), :, :].rearrange("g p n -> (g p) n")

        def t_in_psum(i, m, half):
            if is_first(i, m):
                return psum[:, T0_BANK[half][0]:T0_BANK[half][0] + CHUNKS, 0:HALF]
            return psum[:, T_BANK[half], :].rearrange("p (c n) -> p c n", c=CHUNKS)

        def passes(high, low, moving_high, moving_low):
            return ((high, moving_high), (high, moving_low), (low, moving_high))

        def low_last(high, low, moving_high, moving_low):
            return ([(high, mv, c) for c in range(CHUNKS) for mv in (moving_high, moving_low)]
                    + [(low, moving_high, c) for c in range(CHUNKS)])

        block = ctx.enter_context(nc.Block())

        @block.sync
        def _(sp):
            def load_x(i, m):
                sp.dma_start(xin[:, m % 2].rearrange("p k f -> p (k f)"), graph(x, i, m)).then_inc(x_in[m % 2], 16)

            def store_last(part, blocks):
                cols = slice(blocks[0] * FEATURES, (blocks[-1] + 1) * FEATURES)
                sp.dma_start(out[GRAPHS - 1, :, cols],
                             yout[:, (GRAPHS - 1) % 2, blocks[0]:blocks[-1] + 1, :].rearrange("p k f -> p (k f)")
                             ).then_inc(last_stored[part], 16)

            def load_adj(i, m):
                sp.dma_start(adj[:, m % 2].rearrange("p k n -> p (k n)"), graph(adj_t, i, m)).then_inc(adj_in[m % 2], 16)

            for k in range(BLOCKS):
                sp.dma_start(xin[:, 0, k, :], x[0, :, k * FEATURES:(k + 1) * FEATURES]).then_inc(x0_in[k], 16)
                sp.dma_start(adj[:, 0, k, :], adj_t[0, :, k * NODES:(k + 1) * NODES]).then_inc(adj0_in[k], 16)
            for tile, dram, loaded in ((w0_f, w0, w0_in), (wk_f, wk, wk_in), (wq_f, wq_bq, wq_in), (wv_f, wv_t, wv_in)):
                sp.dma_start(tile[:, :, :].rearrange("p k f -> p (k f)"), dram).then_inc(loaded, 16)
            sp.dma_start(ident[:, :], identity).then_inc(id_in, 16)
            sp.dma_start(bkr[:, :, :].rearrange("p k f -> p (k f)"), bk_rep).then_inc(bk_in, 16)
            sp.dma_start(bqr[:, :, :].rearrange("p k f -> p (k f)"), bq_rep).then_inc(bqr_in, 16)
            sp.dma_start(bv[:, :], bv_rep).then_inc(bv_in, 16)
            load_x(0, 1)
            load_adj(0, 1)

            def turn(i, m):
                if exists(i, m) and exists(i, m + 2):
                    reach(sp, r_out, i, m, 2, 2)
                    load_x(i, m + 2)
                if exists(i, m - 1):
                    if is_last(i, m - 1):
                        for k in (2, 3):
                            sp.wait_ge(norm_out_dve, k - 1)
                            store_last(k - 1, (k,))
                    else:
                        reach(sp, norm_out, i, m - 1, 2, 2)
                        sp.dma_start(graph(out, i, m - 1), yout[:, (m - 1) % 2].rearrange("p k f -> p (k f)")
                                     ).then_inc(stored[(m - 1) % 2], 16)
                if exists(i, m) and exists(i, m + 2):
                    reach(sp, wgt_out, i, m, 4, 4)
                    load_adj(i, m + 2)
                if is_last(i, m):
                    sp.wait_ge(norm_out, 2 * GRAPHS - 1)
                    store_last(0, (0, 1))

            each_turn(sp, turn)
            sp.wait_ge(stored[0], 16 * GRAPHS // 2)
            sp.wait_ge(stored[1], 16 * (GRAPHS // 2 - 1))
            for part in range(3):
                sp.wait_ge(last_stored[part], 16)

        @block.tensor
        def _(pe):
            def fold_weights():
                pe.wait_ge(wk_in, 16)
                pe.wait_ge(wq_in, 16)
                for c in range(CHUNKS):
                    for o in range(CHUNKS):
                        last = nc.tensor.matmul(psum[:, FOLD_BANK[c], 0:VCOLS], wk_f[:, o, c * P:(c + 1) * P],
                                                wq_f[:, o, :], start=(o == 0), stop=(o == CHUNKS - 1))
                last.then_inc(fold_mm, 1)

            def fold_biases():
                pe.wait_ge(bk_in, 16)
                pe.wait_ge(bqr_in, 16)
                for c in range(CHUNKS):
                    for o in range(CHUNKS):
                        nc.tensor.matmul(psum[:, BIAS_BANK, c * COPIES:(c + 1) * COPIES], wq_f[:, o, c * P:(c + 1) * P],
                                         bkr[:, o, :], start=(o == 0), stop=(o == CHUNKS - 1))
                for o in range(CHUNKS):
                    last = nc.tensor.matmul(psum[:, BIAS_BANK, CHUNKS * COPIES:(CHUNKS + 1) * COPIES], bqr[:, o, :],
                                            bkr[:, o, :], start=(o == 0), stop=(o == CHUNKS - 1))
                last.then_inc(bias_mm, 1)

            def make_y(i, m):
                def add_high(fo, c):
                    for w in (wqk_h, wqk_l):
                        nc.tensor.matmul(psum[:, Y_BANK[fo], :], w[:, c, fo * P:(fo + 1) * P], x1t_h[:, c, :],
                                         start=(c == 0 and w is wqk_h), stop=False)

                def add_low(fo, c):
                    return nc.tensor.matmul(psum[:, Y_BANK[fo], :], wqk_h[:, c, fo * P:(fo + 1) * P], x1t_l[:, c, :],
                                            start=False, stop=(c == CHUNKS - 1))

                for c in range(CHUNKS):
                    reach(pe, x1th_out, i, m, 2, c + 1)
                    add_high(0, c)
                add_high(1, 0)
                for c in range(CHUNKS):
                    reach(pe, x1tl_out, i, m, 2, c + 1)
                    last = add_low(0, c)
                last.then_inc(y_mm, 1)
                add_high(1, 1)
                for c in range(CHUNKS):
                    last = add_low(1, c)
                last.then_inc(y_mm, 1)

            def make_v(i, m):
                reach(pe, u_out, i, m - 1, 4, 4)
                for k in range(BLOCKS):
                    rows = slice(k * P, (k + 1) * P)
                    for n, (st, mv, c) in enumerate(low_last(x1t_h, x1t_l, wv_h, wv_l)):
                        last = nc.tensor.matmul(psum[:, V_BANK + k, 0:VCOLS], st[:, c, rows], mv[:, c, :],
                                                start=(n == 0), stop=(n == 3 * CHUNKS - 1))
                    if k % 2:
                        last.then_inc(v_mm, 1)

            def make_scores(i, m):
                reach(pe, yh_out, i, m, 2, 2)
                reach(pe, yl_out, i, m, 2, 2)
                for k in range(BLOCKS):
                    rows = slice(k * P, (k + 1) * P)
                    for n, (st, mv, c) in enumerate(low_last(y_h, y_l, x1t_h, x1t_l)):
                        last = nc.tensor.matmul(psum[:, S_BANK[k], :], st[:, c, rows], mv[:, c, :],
                                                start=(n == 0), stop=(n == 3 * CHUNKS - 1))
                    last.then_inc(s_mm, 1)

            def add_to_t(bank, parity, half, f, k):
                nodes = slice(half * HALF, (half + 1) * HALF)
                cols = slice(f * P, (f + 1) * P)
                for n, (st, mv) in enumerate(passes(x_h, x_l, adj_h, adj_l)):
                    last = nc.tensor.matmul(bank, st[:, parity, k, cols], mv[:, k, nodes],
                                            start=(k == 0 and n == 0), stop=(k == BLOCKS - 1 and n == 2))
                return last

            def make_t(i, m):
                if is_first(i, m):
                    for k, halves in ((0, (0, 1)), (1, (0, 1)), (2, (0,)), (3, (0,)), (2, (1,)), (3, (1,))):
                        pe.wait_ge(x0h_out, k + 1)
                        pe.wait_ge(x0l_out, k + 1)
                        pe.wait_ge(adjh_out, k + 1)
                        pe.wait_ge(adjl_out, k + 1)
                        for half in halves:
                            for f in range(CHUNKS):
                                last = add_to_t(psum[:, T0_BANK[half][f], 0:HALF], 0, half, f, k)
                            if k == BLOCKS - 1:
                                last.then_inc(t_mm, 1)
                else:
                    reach(pe, xh_out, i, m, 1, 0)
                    reach(pe, xl_out, i, m, 1, 0)
                    reach(pe, vl_out, i, m - 1, 2, 2)
                    for half in range(2):
                        for f in range(CHUNKS):
                            for k in range(BLOCKS):
                                if half == 0 and f == 0:
                                    reach(pe, adjh_out, i, m, 4, k + 1)
                                    reach(pe, adjl_out, i, m, 4, k + 1)
                                last = add_to_t(psum[:, T_BANK[half], f * HALF:(f + 1) * HALF], m % 2, half, f, k)
                        last.then_inc(t_mm, 1)

            def make_o(i, m):
                for half in range(2):
                    reach(pe, th_out, i, m, 2, half + 1)
                    for k in range(2):
                        rows = slice(k * P, (k + 1) * P)
                        for n, (st, mv, c) in enumerate(low_last(t_h, t_l, w0_h, w0_l)):
                            if k == 0 and n == 2 * CHUNKS:
                                reach(pe, tl_out, i, m, 2, half + 1)
                            last = nc.tensor.matmul(psum[:, O_BANK[half], k * FEATURES:(k + 1) * FEATURES],
                                                    st[:, half, c, rows], mv[:, c, :],
                                                    start=(n == 0), stop=(n == 3 * CHUNKS - 1))
                    last.then_inc(o_mm, 1)

            def make_attention(i, m, queries, keys=range(BLOCKS)):
                if queries[0] == 0:
                    reach(pe, vh_out, i, m, 2, 2)
                    reach(pe, vl_out, i, m, 2, 2)
                for k in keys:
                    if queries[0] == 0:
                        reach(pe, wgth_out, i, m, 4, k + 1)
                        reach(pe, wgtl_out, i, m, 4, k + 1)
                    for q in queries:
                        for n, (st, mv) in enumerate(passes(wgt_h, wgt_l, v_h, v_l)):
                            last = nc.tensor.matmul(psum[:, Q_BANK[q], 0:VCOLS], st[:, k, q * P:(q + 1) * P], mv[:, k, :],
                                                    start=(k == 0 and n == 0), stop=(k == BLOCKS - 1 and n == 2))
                        if k == BLOCKS - 1:
                            last.then_inc(q_mm, 1)

            def make_x1t(i, m, half):
                reach(pe, x1_out, i, m, 2, half + 1)
                for c in range(CHUNKS):
                    for k in (2 * half, 2 * half + 1):
                        if c == 0 and k % 2:
                            reach(pe, x1_out_act, i, m, 2, half + 1)
                        last = nc.tensor.transpose(psum[:, X1T_BANK[c], k * P:(k + 1) * P],
                                                   x1[:, k, c * P:(c + 1) * P], ident[:, :])
                    if half == 1:
                        last.then_inc(x1t_mm, 1)

            def keep_warm(products):
                for _ in range(products):
                    nc.tensor.matmul(psum[:, WARM_BANK, 0:HALF], warm[:, 0:P], warm[:, :], start=True, stop=True)

            pe.wait_ge(warm_set, 1)
            keep_warm(19)

            def turn(i, m):
                if exists(i, m):
                    if is_first(i, m):
                        keep_warm(8)
                        pe.wait_ge(wqkh_out, 1)
                        pe.wait_ge(wqkl_out, 1)
                        pe.wait_ge(wvc_out, 1)
                    make_y(i, m)
                    if is_first(i, m):
                        pe.wait_ge(wvh_out, 1)
                        pe.wait_ge(wvl_out, 1)
                    make_v(i, m)
                    make_scores(i, m)
                if exists(i, m + 1):
                    make_t(i, m + 1)
                    if is_first(i, m + 1):
                        pe.wait_ge(w0h_out, 1)
                        pe.wait_ge(w0l_out, 1)
                    make_o(i, m + 1)
                    if is_first(i, m + 1):
                        fold_weights()
                        fold_biases()
                        keep_warm(4)
                if is_last(i, m):
                    make_attention(i, m, range(BLOCKS), (0, 1))
                    make_attention(i, m, (0, 1), (2, 3))
                    make_attention(i, m, (2,), (2, 3))
                    make_attention(i, m, (3,), (2, 3))
                elif exists(i, m):
                    for q in range(3):
                        make_attention(i, m, (q,))
                if exists(i, m + 1):
                    if is_first(i, m + 1):
                        pe.wait_ge(id_in, 16)
                    make_x1t(i, m + 1, 0)
                    if exists(i, m):
                        make_attention(i, m, (3,), (0,))
                    make_x1t(i, m + 1, 1)
                    if exists(i, m):
                        make_attention(i, m, (3,), range(1, BLOCKS))

            each_turn(pe, turn)

        @block.scalar
        def _(act):
            flat = lambda t: t[:, :, :].rearrange("p a b -> p (a b)")
            nc.scalar.preload_act_table(ACT.Exp)

            def split_x(i, m):
                reach_dma(act, x_in, i, m, earlier=(m + 1) % 2)
                nc.scalar.activation(x_h[:, m % 2], xin[:, m % 2], ACT.Copy).then_inc(xh_out, 1)

            def split_adj(i, m, k):
                if k == 0:
                    reach_dma(act, adj_in, i, m, earlier=(m + 1) % 2)
                nc.scalar.activation(adj_h[:, k, :], adj[:, m % 2, k, :], ACT.Copy).then_inc(adjh_out, 1)

            for k in range(BLOCKS):
                act.wait_ge(x0_in[k], 16)
                nc.scalar.activation(x_h[:, 0, k], xin[:, 0, k], ACT.Copy).then_inc(x0h_out, 1)
                act.wait_ge(adj0_in[k], 16)
                nc.scalar.activation(adj_h[:, k, :], adj[:, 0, k, :], ACT.Copy).then_inc(adjh_out, 1)

            def normalise(i, m, pair):
                reach(act, shift2_out, i, m, 2, pair + 1)
                if pair == 0:
                    reach_dma(act, stored, i, m - 2)
                for k in (2 * pair, 2 * pair + 1):
                    last = nc.scalar.activation(yout[:, m % 2, k, :], u[:, k, :], ACT.Identity,
                                                bias=shift2[:, k:k + 1], scale=rstd2[:, k:k + 1])
                last.then_inc(norm_out, 1)

            def turn(i, m):
                now, after = exists(i, m), exists(i, m + 1)
                if after and not is_first(i, m + 1):
                    split_adj(i, m + 1, 0)
                    split_adj(i, m + 1, 1)
                for fo in range(CHUNKS):
                    if now:
                        if is_first(i, m) and fo == 0:
                            act.wait_ge(bias_out, 1)
                        reach(act, y_mm, i, m, 2, fo + 1)
                        nc.scalar.activation(y_h[:, fo, :], psum[:, Y_BANK[fo], :], ACT.Identity,
                                             bias=y_bias[:, fo:fo + 1]).then_inc(yh_out, 1)
                    if after and not is_first(i, m + 1):
                        split_adj(i, m + 1, 2 + fo)
                if is_first(i, m + 1):
                    act.wait_ge(w0_in, 16)
                    nc.scalar.activation(flat(w0_h), flat(w0_f), ACT.Copy).then_inc(w0h_out, 1)
                if now:
                    for pair in range(2):
                        reach(act, v_mm, i, m, 2, pair + 1)
                        nc.scalar.activation(v_h[:, 2 * pair:2 * pair + 2, 0:FEATURES],
                                             psum[:, V_BANK + 2 * pair:V_BANK + 2 * pair + 2, 0:FEATURES],
                                             ACT.Copy).then_inc(vh_out, 1)
                if exists(i, m - 1) and not is_last(i, m):
                    if not is_last(i, m - 1):
                        normalise(i, m - 1, 0)
                        normalise(i, m - 1, 1)

                def split_weights(k):
                    reach(act, wgt_out, i, m, 4, k + 1)
                    nc.scalar.activation(wgt_h[:, k, :], wgt[:, k, :], ACT.Copy).then_inc(wgth_out, 1)

                if now:
                    reach(act, c_out, i, m, 1, 1)
                    for k in range(BLOCKS):
                        reach(act, s_mm, i, m, 4, k + 1)
                        nc.scalar.activation(expo[:, k, :], psum[:, S_BANK[k], :], ACT.Exp,
                                             bias=c_key[:, k:k + 1]).then_inc(exp_out, 1)
                        if k:
                            split_weights(k - 1)
                    split_weights(BLOCKS - 1)
                if after:
                    for half in range(2):
                        reach(act, t_mm, i, m + 1, 2, half + 1)
                        nc.scalar.activation(t_h[:, half], t_in_psum(i, m + 1, half), ACT.Copy).then_inc(th_out, 1)
                        if half == (1 if is_first(i, m + 1) else 0) and exists(i, m + 2):
                            split_x(i, m + 2)
                if is_first(i, m + 1):
                    act.wait_ge(fold_mm, 1)
                    nc.scalar.activation(wqk_h[:, :, :], psum[:, 0:2, 0:FEATURES], ACT.Copy).then_inc(wqkh_out, 1)
                if after:
                    for half in range(2):
                        k = 2 * half + 1
                        reach(act, shift1_out, i, m + 1, 2, half + 1)
                        nc.scalar.activation(x1[:, k, :], r[:, k, :], ACT.Identity, bias=shift1[:, k:k + 1],
                                             scale=mrstd1[:, k:k + 1]).then_inc(x1_out_act, 1)
                if after:
                    for c in range(CHUNKS):
                        reach(act, x1t_mm, i, m + 1, 2, c + 1)
                        nc.scalar.activation(x1t_h[:, c, :], psum[:, X1T_BANK[c], :], ACT.Copy).then_inc(x1th_out, 1)
                if is_first(i, m + 1):
                    act.wait_ge(wvc_out, 1)
                    nc.scalar.activation(flat(wv_h), flat(wv_f), ACT.Copy).then_inc(wvh_out, 1)
                if is_last(i, m):
                    normalise(i, m - 1, 0)
                    normalise(i, m - 1, 1)
                    normalise(i, m, 0)

            each_turn(act, turn)

        @block.vector
        def _(dve):
            flat = lambda t: t[:, :, :].rearrange("p a b -> p (a b)")
            as32 = lambda ap: ap.bitcast(f32)

            nc.vector.memset(as32(warm[:, :]), 0.0).then_inc(warm_set, 1)
            nc.vector.memset(neg_half[:, :], -0.5).then_inc(const_set, 1)
            nc.vector.memset(as32(v_h[:, :, FEATURES:FEATURES + 1]), 1.0)
            nc.vector.memset(as32(v_h[:, :, FEATURES + 1:VCOLS]), 0.0)
            nc.vector.memset(as32(v_l[:, :, FEATURES:VCOLS]), 0.0)

            def find_mask(i, m):
                if is_first(i, m):
                    for k in range(BLOCKS):
                        dve.wait_ge(x0_in[k], 16)
                else:
                    reach_dma(dve, x_in, i, m, earlier=(m + 1) % 2)
                nc.vector.tensor_reduce(xmax[:, :], xin[:, m % 2], AX.X, ALU.max,
                                        apply_absolute_value=True).then_inc(mask_max, 1)
                reach(dve, mask_max, i, m, 1, 1)
                nc.vector.tensor_scalar(mask[:, :], xmax[:, :], 0.0, None, ALU.is_gt).then_inc(mask_out, 1)

            def invert_sums(i, m, queries):
                for q in queries:
                    reach(dve, q_mm, i, m, 4, q + 1)
                    nc.vector.reciprocal(rsum[:, q:q + 1], psum[:, Q_BANK[q], FEATURES:FEATURES + 1]).then_inc(rsum_out, 1)

            def add_attention(i, m, queries):
                if queries[0] == 0:
                    reach(dve, x1b_out, i, m, 1, 1)
                for q in queries:
                    reach(dve, rsum_out, i, m, 4, q + 1)
                    nc.vector.scalar_tensor_tensor(u[:, q, :], psum[:, Q_BANK[q], 0:FEATURES], rsum[:, q:q + 1],
                                                   x1b[:, q, :], ALU.mult, ALU.add).then_inc(u_out, 1)

            def sum_statistics(i, m, queries):
                for q in queries:
                    reach(dve, u_out, i, m, 4, q + 1)
                    nc.vector.bn_stats(stats2[:, q, :], u[:, q, :])

            def find_variances(i, m, pairs):
                dve.drain()
                for pair in pairs:
                    for q in (2 * pair, 2 * pair + 1):
                        last = nc.vector.bn_aggr(mv2[:, q, :], stats2[:, q, :])
                    last.then_inc(mv2_out, 1)
                for pair in pairs:
                    blocks = slice(2 * pair, 2 * pair + 2)
                    reach(dve, mv2_out, i, m, 2, pair + 1)
                    nc.vector.tensor_scalar(var2[:, blocks], mv2[:, blocks, 1], EPS, None, ALU.add).then_inc(var2_out, 1)

            def find_shift(i, m, pair):
                blocks = slice(2 * pair, 2 * pair + 2)
                reach(dve, rstd2_out, i, m, 2, pair + 1)
                nc.vector.scalar_tensor_tensor(shift2[:, blocks], mv2[:, blocks, 0], -1.0, rstd2[:, blocks],
                                               ALU.mult, ALU.mult).then_inc(shift2_out, 1)

            def turn(i, m):
                now, after = exists(i, m), exists(i, m + 1)
                if exists(i, m - 1):
                    if is_last(i, m - 1):
                        invert_sums(i, m - 1, (2, 3))
                        dve.wait_ge(norm_out, 2 * GRAPHS - 2)
                        add_attention(i, m - 1, (2, 3))
                        find_shift(i, m - 1, 0)
                        sum_statistics(i, m - 1, (2, 3))
                        find_variances(i, m - 1, (1,))
                        reach(dve, rstd2_out, i, m - 1, 2, 2)
                        reach_dma(dve, stored, i, m - 3)
                        for k in (2, 3):
                            nc.vector.tensor_scalar(yout[:, (m - 1) % 2, k, :], u[:, k, :], mv2[:, k, 0:1],
                                                    rstd2[:, k:k + 1], ALU.subtract, ALU.mult).then_inc(norm_out_dve, 1)
                    else:
                        invert_sums(i, m - 1, (2, 3))
                        add_attention(i, m - 1, (2, 3))
                        sum_statistics(i, m - 1, (0, 1))
                if is_first(i, m + 1):
                    for k in range(BLOCKS):
                        dve.wait_ge(adjh_out, k + 1)
                        nc.vector.tensor_tensor(adj_l[:, k, :], adj[:, 0, k, :], as32(adj_h[:, k, :]),
                                                ALU.subtract).then_inc(adjl_out, 1)
                for fo in range(CHUNKS):
                    if now:
                        reach(dve, yh_out, i, m, 2, fo + 1)
                        nc.vector.scalar_tensor_tensor(y_l[:, fo, :], psum[:, Y_BANK[fo], :], y_bias[:, fo:fo + 1],
                                                       as32(y_h[:, fo, :]), ALU.add, ALU.subtract).then_inc(yl_out, 1)
                    if exists(i, m - 1) and not is_last(i, m - 1):
                        if fo == 0:
                            sum_statistics(i, m - 1, (2, 3))
                        else:
                            find_variances(i, m - 1, (0, 1))
                if now:
                    for pair in range(2):
                        reach(dve, vh_out, i, m, 2, pair + 1)
                        if pair == 1:
                            nc.vector.tensor_scalar(c_key[:, :], psum[:, V_BANK:V_BANK + BLOCKS, FEATURES],
                                                    bqbk[:, 0:1], None, ALU.add).then_inc(c_out, 1)
                        nc.vector.tensor_tensor(v_l[:, 2 * pair:2 * pair + 2, 0:FEATURES],
                                                psum[:, V_BANK + 2 * pair:V_BANK + 2 * pair + 2, 0:FEATURES],
                                                as32(v_h[:, 2 * pair:2 * pair + 2, 0:FEATURES]),
                                                ALU.subtract).then_inc(vl_out, 1)
                        if exists(i, m - 1) and not is_last(i, m - 1):
                            find_shift(i, m - 1, pair)

                def split_weights(k):
                    reach(dve, wgth_out, i, m, 4, k + 1)
                    nc.vector.tensor_tensor(wgt_l[:, k, :], wgt[:, k, :], as32(wgt_h[:, k, :]),
                                            ALU.subtract).then_inc(wgtl_out, 1)

                if now:
                    for k in range(BLOCKS):
                        reach(dve, exp_out, i, m, 4, k + 1)
                        nc.vector.tensor_tensor(wgt[:, k, :], expo[:, k, :], adj[:, m % 2, k, :],
                                                ALU.mult).then_inc(wgt_out, 1)
                        if k:
                            split_weights(k - 1)
                    split_weights(BLOCKS - 1)
                if after:
                    if is_first(i, m + 1):
                        find_mask(i, m + 1)
                    for half in range(2):
                        reach(dve, th_out, i, m + 1, 2, half + 1)
                        nc.vector.tensor_tensor(t_l[:, half], t_in_psum(i, m + 1, half), as32(t_h[:, half]),
                                                ALU.subtract).then_inc(tl_out, 1)
                        if half == 0 and not is_first(i, m + 1):
                            find_mask(i, m + 1)
                    for half in range(2):
                        blocks = slice(2 * half, 2 * half + 2)
                        reach(dve, o_mm, i, m + 1, 2, half + 1)
                        nc.vector.scalar_tensor_tensor(r[:, blocks, :].rearrange("p k f -> p (k f)"),
                                                       psum[:, O_BANK[half], :], 0.0,
                                                       xin[:, (m + 1) % 2, blocks, :].rearrange("p k f -> p (k f)"),
                                                       ALU.max, ALU.add).then_inc(r_out, 1)
                        reach(dve, r_out, i, m + 1, 2, half + 1)
                        for k in (2 * half, 2 * half + 1):
                            nc.vector.bn_stats(stats1[:, k, :], r[:, k, :])
                        dve.drain()
                        for k in (2 * half, 2 * half + 1):
                            last = nc.vector.bn_aggr(mv1[:, k, :], stats1[:, k, :])
                        last.then_inc(mv1_out, 1)
                        reach(dve, mv1_out, i, m + 1, 2, half + 1)
                        nc.vector.tensor_scalar(var1[:, blocks], mv1[:, blocks, 1], EPS, None, ALU.add).then_inc(var1_out, 1)
                    reach(dve, mask_out, i, m + 1, 1, 1)
                    reach(dve, x1b_out, i, m, 1, 1)
                    for half in range(2):
                        blocks = slice(2 * half, 2 * half + 2)
                        reach(dve, rstd1_out, i, m + 1, 2, half + 1)
                        nc.vector.tensor_tensor(mrstd1[:, blocks], rstd1[:, blocks], mask[:, blocks],
                                                ALU.mult).then_inc(mrstd1_out, 1)
                        reach(dve, mrstd1_out, i, m + 1, 2, half + 1)
                        k = 2 * half
                        nc.vector.scalar_tensor_tensor(shift1[:, k + 1:k + 2], mv1[:, k + 1, 0:1], -1.0,
                                                       mrstd1[:, k + 1:k + 2], ALU.mult, ALU.mult).then_inc(shift1_out, 1)
                        nc.vector.tensor_scalar(x1[:, k, :], r[:, k, :], mv1[:, k, 0:1], mrstd1[:, k:k + 1],
                                                ALU.subtract, ALU.mult).then_inc(x1_out, 1)
                if is_last(i, m):
                    dve.wait_ge(norm_out, 2 * GRAPHS - 3)
                if now:
                    invert_sums(i, m, (0, 1))
                    add_attention(i, m, (0, 1))
                if is_first(i, m + 1):
                    dve.wait_ge(wqkh_out, 1)
                    nc.vector.tensor_tensor(wqk_l[:, :, :], psum[:, 0:2, 0:FEATURES], as32(wqk_h[:, :, :]),
                                            ALU.subtract).then_inc(wqkl_out, 1)
                    dve.wait_ge(wv_in, 16)
                    nc.vector.tensor_copy(wv_f[:, :, FEATURES], psum[:, 0:2, FEATURES]).then_inc(wvc_out, 1)
                if after:
                    for c in range(CHUNKS):
                        reach(dve, x1th_out, i, m + 1, 2, c + 1)
                        nc.vector.tensor_tensor(x1t_l[:, c, :], psum[:, X1T_BANK[c], :], as32(x1t_h[:, c, :]),
                                                ALU.subtract).then_inc(x1tl_out, 1)
                if is_last(i, m):
                    sum_statistics(i, m, (0, 1))
                    find_variances(i, m, (0,))
                if is_first(i, m + 1):
                    dve.wait_ge(bias_mm, 1)
                    nc.vector.tensor_copy(bqbk[:, :], psum[:, BIAS_BANK, CHUNKS * COPIES:CHUNKS * COPIES + 1])
                    nc.vector.tensor_copy(y_bias[:, :], psum[:, BIAS_BANK, 0:CHUNKS * COPIES:COPIES]).then_inc(bias_out, 1)

            each_turn(dve, turn)

        @block.gpsimd
        def _(pool):
            flat = lambda t: t[:, :, :].rearrange("p a b -> p (a b)")
            as32 = lambda ap: ap.bitcast(f32)

            def split_x(i, m):
                reach(pool, xh_out, i, m, 1, 0)
                nc.gpsimd.tensor_tensor(x_l[:, m % 2], xin[:, m % 2], as32(x_h[:, m % 2]),
                                        ALU.subtract).then_inc(xl_out, 1)

            def split_adj(i, m, blocks):
                for k in blocks:
                    reach(pool, adjh_out, i, m, 4, k + 1)
                    nc.gpsimd.tensor_tensor(adj_l[:, k, :], adj[:, m % 2, k, :], as32(adj_h[:, k, :]),
                                            ALU.subtract).then_inc(adjl_out, 1)

            def find_deviation(i, m, pair):
                blocks = slice(2 * pair, 2 * pair + 2)
                reach(pool, var2_out, i, m, 2, pair + 1)
                nc.gpsimd.tensor_tensor(rstd2[:, blocks], var2[:, blocks], neg_half[:, blocks],
                                        ALU.pow).then_inc(rstd2_out, 1)

            for k in range(BLOCKS):
                pool.wait_ge(x0h_out, k + 1)
                nc.gpsimd.tensor_tensor(x_l[:, 0, k], xin[:, 0, k], as32(x_h[:, 0, k]), ALU.subtract).then_inc(x0l_out, 1)
            pool.wait_ge(w0h_out, 1)
            nc.gpsimd.tensor_tensor(flat(w0_l), flat(w0_f), as32(flat(w0_h)), ALU.subtract).then_inc(w0l_out, 1)
            pool.wait_ge(const_set, 1)

            def turn(i, m):
                if exists(i, m + 1) and not is_first(i, m + 1):
                    split_adj(i, m + 1, range(BLOCKS - 1))
                if exists(i, m - 1):
                    if not is_last(i, m - 1):
                        find_deviation(i, m - 1, 0)
                    find_deviation(i, m - 1, 1)
                if exists(i, m + 1) and not is_first(i, m + 1):
                    split_adj(i, m + 1, (BLOCKS - 1,))
                if exists(i, m):
                    if is_first(i, m):
                        pool.wait_ge(bv_in, 16)
                    reach(pool, x1_out, i, m, 2, 2)
                    reach(pool, x1_out_act, i, m, 2, 2)
                    nc.gpsimd.tensor_tensor(x1b[:, :, :], x1[:, :, :],
                                            bv[:, :].unsqueeze(1).to_broadcast([P, BLOCKS, FEATURES]),
                                            ALU.add).then_inc(x1b_out, 1)
                if exists(i, m + 2) and exists(i, m + 1):
                    split_x(i, m + 2)
                if exists(i, m + 1):
                    for half in range(2):
                        blocks = slice(2 * half, 2 * half + 2)
                        reach(pool, var1_out, i, m + 1, 2, half + 1)
                        nc.gpsimd.tensor_tensor(rstd1[:, blocks], var1[:, blocks], neg_half[:, blocks],
                                                ALU.pow).then_inc(rstd1_out, 1)
                if is_first(i, m + 1):
                    pool.wait_ge(wvh_out, 1)
                    nc.gpsimd.tensor_tensor(flat(wv_l), flat(wv_f), as32(flat(wv_h)), ALU.subtract).then_inc(wvl_out, 1)
                if is_last(i, m):
                    find_deviation(i, m, 0)

            each_turn(pool, turn)


def kernel(x, adj, L0_gnn_kernel, L1_gnn_Wq_w, L1_gnn_Wq_b, L1_gnn_Wk_w, L1_gnn_Wk_b, L1_gnn_Wv_w, L1_gnn_Wv_b):
    import numpy as np
    import concourse.bacc as bacc
    from concourse import mybir as mb
    from concourse.bass_utils import run_bass_kernel_spmd

    def by_partition(a):
        a = np.asarray(a)
        *lead, rows, n = a.shape
        a = a.reshape(*lead, rows // P, P, n)
        return np.ascontiguousarray(np.moveaxis(a, -3, -2).reshape(*lead, P, rows // P * n))

    wv_t = np.asarray(L1_gnn_Wv_w).T
    wv_t = np.concatenate([wv_t, np.zeros((FEATURES, VCOLS - FEATURES), wv_t.dtype)], axis=1)
    bq = np.asarray(L1_gnn_Wq_b)[:, None]
    wq_bq = np.concatenate([np.asarray(L1_gnn_Wq_w), bq, np.zeros_like(bq)], axis=1)
    ins = {
        "x": by_partition(x),
        "adj_t": by_partition(np.swapaxes(np.asarray(adj), 1, 2)),
        "w0": by_partition(L0_gnn_kernel),
        "wq_bq": by_partition(wq_bq),
        "wk": by_partition(L1_gnn_Wk_w),
        "wv_t": by_partition(wv_t),
        "bq_rep": by_partition(np.repeat(bq, P, axis=1)),
        "bk_rep": by_partition(np.repeat(np.asarray(L1_gnn_Wk_b)[:, None], COPIES, axis=1)),
        "bv_rep": np.ascontiguousarray(np.repeat(np.asarray(L1_gnn_Wv_b)[None, :], P, axis=0)),
        "identity": np.eye(P, dtype=np.float32),
    }
    nc = bacc.Bacc("TRN2", target_bir_lowering=False, num_devices=1)
    args = [nc.dram_tensor(f"in_{n}", a.shape, mb.dt.from_np(a.dtype), kind="ExternalInput").ap() for n, a in ins.items()]
    out = nc.dram_tensor("out", (GRAPHS, P, BLOCKS * FEATURES), mb.dt.float32, kind="ExternalOutput").ap()
    build(nc, *args, out)
    got = run_bass_kernel_spmd(nc, [{f"in_{n}": a for n, a in ins.items()}], core_ids=[0]).results[0]["out"]
    return np.ascontiguousarray(
        got.reshape(GRAPHS, P, BLOCKS, FEATURES).transpose(0, 2, 1, 3).reshape(GRAPHS, NODES, FEATURES))
```
